# Optimizing a Trainium2 kernel written in Bass

```python
import numpy as np
import jax
import jax.numpy as jnp

def _softmax(x, axis=-1):
    return jax.nn.softmax(x, axis=axis)

def _gelu(x):
    return jax.nn.gelu(x, approximate=True)

def _silu(x):
    return jax.nn.silu(x)

def _sigmoid(x):
    return jax.nn.sigmoid(x)

def _layernorm(x, axis=-1, eps=1e-05):
    m = jnp.mean(x, axis=axis, keepdims=True)
    v = jnp.var(x, axis=axis, keepdims=True)
    return (x - m) / jnp.sqrt(v + eps)

def _scatter_add(tgt, idx, src, axis=0):
    return tgt.at[idx].add(src)

def _segment_sum(src, seg, n):
    return jax.ops.segment_sum(src, seg, n)
kernel_name = 'mk_recurrent_d2_jaxref_r8_0c68e0'

def setup_inputs(seed: int=0):
    np.random.seed(seed)
    _w = jnp.asarray

    def _L0_attn_setup():
        import jax, jax.numpy as jnp
        import numpy as np
        LN_EPS = 1e-05

        def _layer_norm(c, ln_w, ln_b):
            mu = jnp.mean(c, axis=-1, keepdims=True)
            var = jnp.mean(jnp.square(c - mu), axis=-1, keepdims=True)
            return (c - mu) * jax.lax.rsqrt(var + LN_EPS) * ln_w + ln_b
        key = jax.random.key(seed)
        k_x, k_w, k_b, k_g, k_beta = jax.random.split(key, 5)
        B, S, D, H = (8, 256, 128, 128)
        x = jax.random.normal(k_x, (B, S, D), dtype=jnp.float32)
        W = jax.random.normal(k_w, (4 * H, D), dtype=jnp.float32) * (1.0 / np.sqrt(D))
        b = jax.random.normal(k_b, (4 * H,), dtype=jnp.float32) * 0.01
        ln_w = jnp.ones((H,), dtype=jnp.float32) + 0.01 * jax.random.normal(k_g, (H,), dtype=jnp.float32)
        ln_b = 0.01 * jax.random.normal(k_beta, (H,), dtype=jnp.float32)
        return {'x': x, 'W': W, 'b': b, 'ln_w': ln_w, 'ln_b': ln_b}
    _L0_attn_in = _L0_attn_setup()

    def _L0_ffn_setup():
        import jax, jax.numpy as jnp
        import numpy as np
        D = 128
        P = 4
        DEPTH = 5
        FAN = 4
        G = (FAN ** (DEPTH + 1) - 1) // 3
        N_NODES = G * FAN
        HID = P * N_NODES
        key = jax.random.key(seed)
        k0, k1, k2, k3 = jax.random.split(key, 4)
        return {'oldx': jax.random.normal(k0, (2, 256, D), dtype=jnp.float32), 'W_in': jax.random.normal(k1, (HID, D), dtype=jnp.float32) * (1.0 / np.sqrt(D)), 'b_in': jax.random.normal(k2, (HID,), dtype=jnp.float32) * (1.0 / np.sqrt(D)), 'W_out': jax.random.normal(k3, (D, HID), dtype=jnp.float32) * (1.0 / np.sqrt((DEPTH + 1) * P))}
    _L0_ffn_in = _L0_ffn_setup()

    def _L1_attn_setup():
        import jax, jax.numpy as jnp
        import numpy as np
        B, T, H, NH = (2, 256, 128, 16)
        D = H // NH
        K_CONV = 4

        def _dwconv_silu(x, w):
            Kc = w.shape[1]
            xp = jnp.pad(x, ((0, 0), (Kc - 1, 0), (0, 0))).transpose(0, 2, 1)
            y = jax.lax.conv_general_dilated(xp, w[:, None, :], (1,), 'VALID', feature_group_count=w.shape[0], dimension_numbers=('NCH', 'OIH', 'NCH'))
            return jax.nn.silu(y.transpose(0, 2, 1))

        def _l2norm(x, eps=1e-06):
            return x * jax.lax.rsqrt(jnp.sum(x * x, -1, keepdims=True) + eps)

        def _forward(hidden, Wq, Wk, Wv, conv_q, conv_k, conv_v, Wb, Wa, A_log, dt_bias, Wg, norm_w, Wo):
            Bh, Tt, Hh = hidden.shape
            nh = A_log.shape[0]
            d = Hh // nh
            q = _dwconv_silu(hidden @ Wq.T, conv_q).reshape(Bh, Tt, nh, d)
            k = _dwconv_silu(hidden @ Wk.T, conv_k).reshape(Bh, Tt, nh, d)
            v = _dwconv_silu(hidden @ Wv.T, conv_v).reshape(Bh, Tt, nh, d)
            q = _l2norm(q) * d ** (-0.5)
            k = _l2norm(k)
            beta = jax.nn.sigmoid(hidden @ Wb.T)
            g = -jnp.exp(A_log) * jax.nn.softplus(hidden @ Wa.T + dt_bias)

            def step(S, inp):
                qt, kt, vt, gt, bt = inp
                S = S * jnp.exp(gt)[..., None, None]
                pred = jnp.einsum('bhk,bhkv->bhv', kt, S)
                dv = (vt - pred) * bt[..., None]
                S = S + jnp.einsum('bhk,bhv->bhkv', kt, dv)
                ot = jnp.einsum('bhk,bhkv->bhv', qt, S)
                return (S, ot)
            xs = (q.transpose(1, 0, 2, 3), k.transpose(1, 0, 2, 3), v.transpose(1, 0, 2, 3), g.transpose(1, 0, 2), beta.transpose(1, 0, 2))
            S0 = jnp.zeros((Bh, nh, d, d), hidden.dtype)
            _, o = jax.lax.scan(step, S0, xs)
            o = o.transpose(1, 0, 2, 3)
            gate = (hidden @ Wg.T).reshape(Bh, Tt, nh, d)
            o = o * jax.lax.rsqrt(jnp.mean(o * o, -1, keepdims=True) + 1e-05) * norm_w
            o = o * jax.nn.silu(gate)
            return o.reshape(Bh, Tt, Hh) @ Wo.T
        key = jax.random.key(seed)
        ks = jax.random.split(key, 16)
        s = 0.02
        return {'hidden': jax.random.normal(ks[0], (B, T, H), jnp.float32), 'Wq': jax.random.normal(ks[1], (H, H), jnp.float32) * s, 'Wk': jax.random.normal(ks[2], (H, H), jnp.float32) * s, 'Wv': jax.random.normal(ks[3], (H, H), jnp.float32) * s, 'conv_q': jax.random.normal(ks[4], (H, K_CONV), jnp.float32) * 0.5, 'conv_k': jax.random.normal(ks[5], (H, K_CONV), jnp.float32) * 0.5, 'conv_v': jax.random.normal(ks[6], (H, K_CONV), jnp.float32) * 0.5, 'Wb': jax.random.normal(ks[7], (NH, H), jnp.float32) * s, 'Wa': jax.random.normal(ks[8], (NH, H), jnp.float32) * s, 'A_log': jnp.log(jax.random.uniform(ks[9], (NH,), jnp.float32, 1.0, 16.0)), 'dt_bias': jnp.log(jnp.expm1(jax.random.uniform(ks[10], (NH,), jnp.float32, 0.001, 0.1))), 'Wg': jax.random.normal(ks[11], (H, H), jnp.float32) * s, 'norm_w': jnp.ones((D,), jnp.float32), 'Wo': jax.random.normal(ks[12], (H, H), jnp.float32) * s}
    _L1_attn_in = _L1_attn_setup()

    def _L1_ffn_setup():
        import jax, jax.numpy as jnp
        import numpy as np
        DIM = 128
        DEPTH = 2
        HEADS = 8
        DIM_HEAD = 64
        WINDOW = 64
        INNER = HEADS * DIM_HEAD
        HID = int(DIM * 4 * 2 / 3)
        B, N = (2, 1024)
        QK_SCALE = 8.0

        def shift_token(t):
            t1, t2 = jnp.split(t, 2, axis=-1)
            t2 = jnp.pad(t2, ((0, 0), (1, 0), (0, 0)))[:, :-1]
            return jnp.concatenate([t1, t2], axis=-1)

        def l2norm(t):
            return t / jnp.clip(jnp.linalg.norm(t, axis=-1, keepdims=True), 1e-12)

        def rotate_half(x):
            x1, x2 = jnp.split(x, 2, axis=-1)
            return jnp.concatenate([-x2, x1], axis=-1)

        def rotary_xpos(q, k):
            n = q.shape[-2]
            half_idx = jnp.arange(0, DIM_HEAD, 2, dtype=jnp.float32)
            inv_freq = 1.0 / 10000.0 ** (half_idx / DIM_HEAD)
            t = jnp.arange(n, dtype=jnp.float32)
            freqs = t[:, None] * inv_freq[None, :]
            freqs = jnp.concatenate([freqs, freqs], axis=-1)
            base = (half_idx + 0.4 * DIM_HEAD) / (1.4 * DIM_HEAD)
            power = (t - n // 2) / float(WINDOW // 2)
            scale = base[None, :] ** power[:, None]
            scale = jnp.concatenate([scale, scale], axis=-1)
            cos, sin = (jnp.cos(freqs), jnp.sin(freqs))
            q = q * cos * scale + rotate_half(q) * sin * scale
            k = k * cos / scale + rotate_half(k) * sin / scale
            return (q, k)

        def local_attention(q, k, v):
            b, h, n, d = q.shape
            w = n // WINDOW
            bq = q.reshape(b, h, w, WINDOW, d) * QK_SCALE
            bk = k.reshape(b, h, w, WINDOW, d)
            bv = v.reshape(b, h, w, WINDOW, d)

            def look_around(t):
                p = jnp.pad(t, ((0, 0), (0, 0), (1, 0), (0, 0), (0, 0)))
                return jnp.concatenate([p[:, :, :w], p[:, :, 1:]], axis=3)
            bk, bv = (look_around(bk), look_around(bv))
            bt = jnp.arange(n).reshape(w, WINDOW)
            btp = jnp.pad(bt, ((1, 0), (0, 0)), constant_values=-1)
            btk = jnp.concatenate([btp[:w], btp[1:]], axis=1)
            sim = jnp.einsum('bhwid,bhwjd->bhwij', bq, bk)
            i = bt[:, :, None]
            j = btk[:, None, :]
            mask = (i < j) | (i > j + WINDOW) | (j == -1)
            sim = jnp.where(mask, -jnp.finfo(sim.dtype).max, sim)
            attn = jax.nn.softmax(sim, axis=-1)
            out = jnp.einsum('bhwij,bhwjd->bhwid', attn, bv)
            return out.reshape(b, h, n, d)

        def _layer(x, wqkv, qs, ksc, wo, lg, lb, w1, b1, w2, b2):
            b, n, _ = x.shape
            h = shift_token(x)
            qkv = h @ wqkv
            q, k, v = jnp.split(qkv, 3, axis=-1)
            to_heads = lambda t: t.reshape(b, n, HEADS, DIM_HEAD).transpose(0, 2, 1, 3)
            q, k, v = (to_heads(q), to_heads(k), to_heads(v))
            q = l2norm(q) * qs
            k = l2norm(k) * ksc
            q, k = rotary_xpos(q, k)
            o = local_attention(q, k, v)
            o = o.transpose(0, 2, 1, 3).reshape(b, n, INNER)
            x = x + o @ wo
            h = shift_token(x)
            mu = h.mean(-1, keepdims=True)
            var = h.var(-1, keepdims=True)
            h = (h - mu) / jnp.sqrt(var + 1e-05) * lg + lb
            h = h @ w1 + b1
            a, g = jnp.split(h, 2, axis=-1)
            h = a * jax.nn.gelu(g, approximate=False)
            x = x + h @ w2 + b2
            return x
        key = jax.random.key(seed)
        ks = jax.random.split(key, 6)
        return {'x': jax.random.normal(ks[0], (B, N, DIM), jnp.float32), 'wqkv': jax.random.normal(ks[1], (DEPTH, DIM, 3 * INNER), jnp.float32) * 0.02, 'q_scale': jnp.ones((DEPTH, DIM_HEAD), jnp.float32), 'k_scale': jnp.ones((DEPTH, DIM_HEAD), jnp.float32), 'wo': jax.random.normal(ks[2], (DEPTH, INNER, DIM), jnp.float32) * 0.02, 'ln_g': jnp.ones((DEPTH, DIM), jnp.float32), 'ln_b': jnp.zeros((DEPTH, DIM), jnp.float32), 'w1': jax.random.normal(ks[3], (DEPTH, DIM, 2 * HID), jnp.float32) * 0.02, 'b1': jnp.zeros((DEPTH, 2 * HID), jnp.float32), 'w2': jax.random.normal(ks[4], (DEPTH, HID, DIM), jnp.float32) * 0.02, 'b2': jnp.zeros((DEPTH, DIM), jnp.float32)}
    _L1_ffn_in = _L1_ffn_setup()
    _d = {'L0_attn_x': _L0_attn_in['x'], 'L0_attn_W': _L0_attn_in['W'], 'L0_attn_b': _L0_attn_in['b'], 'L0_attn_ln_w': _L0_attn_in['ln_w'], 'L0_attn_ln_b': _L0_attn_in['ln_b'], 'L0_ffn_W_in': _L0_ffn_in['W_in'], 'L0_ffn_b_in': _L0_ffn_in['b_in'], 'L0_ffn_W_out': _L0_ffn_in['W_out'], 'L1_attn_Wq': _L1_attn_in['Wq'], 'L1_attn_Wk': _L1_attn_in['Wk'], 'L1_attn_Wv': _L1_attn_in['Wv'], 'L1_attn_conv_q': _L1_attn_in['conv_q'], 'L1_attn_conv_k': _L1_attn_in['conv_k'], 'L1_attn_conv_v': _L1_attn_in['conv_v'], 'L1_attn_Wb': _L1_attn_in['Wb'], 'L1_attn_Wa': _L1_attn_in['Wa'], 'L1_attn_A_log': _L1_attn_in['A_log'], 'L1_attn_dt_bias': _L1_attn_in['dt_bias'], 'L1_attn_Wg': _L1_attn_in['Wg'], 'L1_attn_norm_w': _L1_attn_in['norm_w'], 'L1_attn_Wo': _L1_attn_in['Wo'], 'L1_ffn_wqkv': _L1_ffn_in['wqkv'], 'L1_ffn_q_scale': _L1_ffn_in['q_scale'], 'L1_ffn_k_scale': _L1_ffn_in['k_scale'], 'L1_ffn_wo': _L1_ffn_in['wo'], 'L1_ffn_ln_g': _L1_ffn_in['ln_g'], 'L1_ffn_ln_b': _L1_ffn_in['ln_b'], 'L1_ffn_w1': _L1_ffn_in['w1'], 'L1_ffn_b1': _L1_ffn_in['b1'], 'L1_ffn_w2': _L1_ffn_in['w2'], 'L1_ffn_b2': _L1_ffn_in['b2']}
    _x0 = _d['L0_attn_x']
    _d['L0_attn_x'] = jax.random.normal(jax.random.fold_in(jax.random.key(seed), 1), (16, 256, 128), dtype=_x0.dtype)
    del _x0
    return _d

def reference(L0_attn_x, L0_attn_W, L0_attn_b, L0_attn_ln_w, L0_attn_ln_b, L0_ffn_W_in, L0_ffn_b_in, L0_ffn_W_out, L1_attn_Wq, L1_attn_Wk, L1_attn_Wv, L1_attn_conv_q, L1_attn_conv_k, L1_attn_conv_v, L1_attn_Wb, L1_attn_Wa, L1_attn_A_log, L1_attn_dt_bias, L1_attn_Wg, L1_attn_norm_w, L1_attn_Wo, L1_ffn_wqkv, L1_ffn_q_scale, L1_ffn_k_scale, L1_ffn_wo, L1_ffn_ln_g, L1_ffn_ln_b, L1_ffn_w1, L1_ffn_b1, L1_ffn_w2, L1_ffn_b2):

    def _L0_attn_ref(x, W, b, ln_w, ln_b):
        import jax, jax.numpy as jnp
        import numpy as np
        LN_EPS = 1e-05

        def _layer_norm(c, ln_w, ln_b):
            mu = jnp.mean(c, axis=-1, keepdims=True)
            var = jnp.mean(jnp.square(c - mu), axis=-1, keepdims=True)
            return (c - mu) * jax.lax.rsqrt(var + LN_EPS) * ln_w + ln_b
        B, S, D = x.shape
        H = W.shape[0] // 4
        gates = jnp.einsum('bsd,gd->bsg', x, W) + b
        f, i, o, z_raw = jnp.split(gates, 4, axis=-1)
        f = jax.nn.sigmoid(f)
        i = jax.nn.sigmoid(i)
        o = jax.nn.sigmoid(o)
        z = jnp.tanh(z_raw)

        def step(c, fioz_t):
            f_t, i_t, o_t, z_t = fioz_t
            c = f_t * c + i_t * z_t
            h = o_t * jnp.tanh(_layer_norm(c, ln_w, ln_b))
            return (c, h)
        c0 = jnp.zeros((B, H), dtype=x.dtype)
        fs = jnp.swapaxes(f, 0, 1)
        is_ = jnp.swapaxes(i, 0, 1)
        os_ = jnp.swapaxes(o, 0, 1)
        zs = jnp.swapaxes(z, 0, 1)
        _, h_seq = jax.lax.scan(step, c0, (fs, is_, os_, zs))
        return jnp.swapaxes(h_seq, 0, 1)

    def _L0_ffn_ref(oldx, W_in, b_in, W_out):
        import jax, jax.numpy as jnp
        import numpy as np
        D = 128
        P = 4
        DEPTH = 5
        FAN = 4
        G = (FAN ** (DEPTH + 1) - 1) // 3
        N_NODES = G * FAN
        HID = P * N_NODES
        x = oldx.reshape(-1, D)
        B = x.shape[0]
        logits = x @ W_in.T + b_in
        act = jax.nn.gelu(logits, approximate=False)
        act4 = act.reshape(B, P, G, FAN)
        decisions = jnp.argmax(act4, axis=-1)
        current = jnp.zeros((B, P), dtype=jnp.int32)
        nodes = [current]
        platform = 0
        for d in range(DEPTH):
            moves = jnp.take_along_axis(decisions, current[..., None].astype(jnp.int64), axis=2)[..., 0].astype(jnp.int32)
            next_platform = platform + FAN ** d
            current = next_platform + FAN * (current - platform) + moves
            nodes.append(current)
            platform = next_platform
        mask = sum((jax.nn.one_hot(n, G, dtype=act4.dtype) for n in nodes))
        mask = jax.lax.stop_gradient(mask)
        masked = act4 * mask[..., None]
        new_logits = masked.reshape(B, HID) @ W_out.T
        return new_logits.reshape(oldx.shape)

    def _L1_attn_ref(hidden, Wq, Wk, Wv, conv_q, conv_k, conv_v, Wb, Wa, A_log, dt_bias, Wg, norm_w, Wo):
        import jax, jax.numpy as jnp
        import numpy as np
        B, T, H, NH = (2, 256, 128, 16)
        D = H // NH
        K_CONV = 4

        def _dwconv_silu(x, w):
            Kc = w.shape[1]
            xp = jnp.pad(x, ((0, 0), (Kc - 1, 0), (0, 0))).transpose(0, 2, 1)
            y = jax.lax.conv_general_dilated(xp, w[:, None, :], (1,), 'VALID', feature_group_count=w.shape[0], dimension_numbers=('NCH', 'OIH', 'NCH'))
            return jax.nn.silu(y.transpose(0, 2, 1))

        def _l2norm(x, eps=1e-06):
            return x * jax.lax.rsqrt(jnp.sum(x * x, -1, keepdims=True) + eps)

        def _forward(hidden, Wq, Wk, Wv, conv_q, conv_k, conv_v, Wb, Wa, A_log, dt_bias, Wg, norm_w, Wo):
            Bh, Tt, Hh = hidden.shape
            nh = A_log.shape[0]
            d = Hh // nh
            q = _dwconv_silu(hidden @ Wq.T, conv_q).reshape(Bh, Tt, nh, d)
            k = _dwconv_silu(hidden @ Wk.T, conv_k).reshape(Bh, Tt, nh, d)
            v = _dwconv_silu(hidden @ Wv.T, conv_v).reshape(Bh, Tt, nh, d)
            q = _l2norm(q) * d ** (-0.5)
            k = _l2norm(k)
            beta = jax.nn.sigmoid(hidden @ Wb.T)
            g = -jnp.exp(A_log) * jax.nn.softplus(hidden @ Wa.T + dt_bias)

            def step(S, inp):
                qt, kt, vt, gt, bt = inp
                S = S * jnp.exp(gt)[..., None, None]
                pred = jnp.einsum('bhk,bhkv->bhv', kt, S)
                dv = (vt - pred) * bt[..., None]
                S = S + jnp.einsum('bhk,bhv->bhkv', kt, dv)
                ot = jnp.einsum('bhk,bhkv->bhv', qt, S)
                return (S, ot)
            xs = (q.transpose(1, 0, 2, 3), k.transpose(1, 0, 2, 3), v.transpose(1, 0, 2, 3), g.transpose(1, 0, 2), beta.transpose(1, 0, 2))
            S0 = jnp.zeros((Bh, nh, d, d), hidden.dtype)
            _, o = jax.lax.scan(step, S0, xs)
            o = o.transpose(1, 0, 2, 3)
            gate = (hidden @ Wg.T).reshape(Bh, Tt, nh, d)
            o = o * jax.lax.rsqrt(jnp.mean(o * o, -1, keepdims=True) + 1e-05) * norm_w
            o = o * jax.nn.silu(gate)
            return o.reshape(Bh, Tt, Hh) @ Wo.T
        return _forward(hidden, Wq, Wk, Wv, conv_q, conv_k, conv_v, Wb, Wa, A_log, dt_bias, Wg, norm_w, Wo)

    def _L1_ffn_ref(x, wqkv, q_scale, k_scale, wo, ln_g, ln_b, w1, b1, w2, b2):
        import jax, jax.numpy as jnp
        import numpy as np
        DIM = 128
        DEPTH = 2
        HEADS = 8
        DIM_HEAD = 64
        WINDOW = 64
        INNER = HEADS * DIM_HEAD
        HID = int(DIM * 4 * 2 / 3)
        B, N = (2, 1024)
        QK_SCALE = 8.0

        def shift_token(t):
            t1, t2 = jnp.split(t, 2, axis=-1)
            t2 = jnp.pad(t2, ((0, 0), (1, 0), (0, 0)))[:, :-1]
            return jnp.concatenate([t1, t2], axis=-1)

        def l2norm(t):
            return t / jnp.clip(jnp.linalg.norm(t, axis=-1, keepdims=True), 1e-12)

        def rotate_half(x):
            x1, x2 = jnp.split(x, 2, axis=-1)
            return jnp.concatenate([-x2, x1], axis=-1)

        def rotary_xpos(q, k):
            n = q.shape[-2]
            half_idx = jnp.arange(0, DIM_HEAD, 2, dtype=jnp.float32)
            inv_freq = 1.0 / 10000.0 ** (half_idx / DIM_HEAD)
            t = jnp.arange(n, dtype=jnp.float32)
            freqs = t[:, None] * inv_freq[None, :]
            freqs = jnp.concatenate([freqs, freqs], axis=-1)
            base = (half_idx + 0.4 * DIM_HEAD) / (1.4 * DIM_HEAD)
            power = (t - n // 2) / float(WINDOW // 2)
            scale = base[None, :] ** power[:, None]
            scale = jnp.concatenate([scale, scale], axis=-1)
            cos, sin = (jnp.cos(freqs), jnp.sin(freqs))
            q = q * cos * scale + rotate_half(q) * sin * scale
            k = k * cos / scale + rotate_half(k) * sin / scale
            return (q, k)

        def local_attention(q, k, v):
            b, h, n, d = q.shape
            w = n // WINDOW
            bq = q.reshape(b, h, w, WINDOW, d) * QK_SCALE
            bk = k.reshape(b, h, w, WINDOW, d)
            bv = v.reshape(b, h, w, WINDOW, d)

            def look_around(t):
                p = jnp.pad(t, ((0, 0), (0, 0), (1, 0), (0, 0), (0, 0)))
                return jnp.concatenate([p[:, :, :w], p[:, :, 1:]], axis=3)
            bk, bv = (look_around(bk), look_around(bv))
            bt = jnp.arange(n).reshape(w, WINDOW)
            btp = jnp.pad(bt, ((1, 0), (0, 0)), constant_values=-1)
            btk = jnp.concatenate([btp[:w], btp[1:]], axis=1)
            sim = jnp.einsum('bhwid,bhwjd->bhwij', bq, bk)
            i = bt[:, :, None]
            j = btk[:, None, :]
            mask = (i < j) | (i > j + WINDOW) | (j == -1)
            sim = jnp.where(mask, -jnp.finfo(sim.dtype).max, sim)
            attn = jax.nn.softmax(sim, axis=-1)
            out = jnp.einsum('bhwij,bhwjd->bhwid', attn, bv)
            return out.reshape(b, h, n, d)

        def _layer(x, wqkv, qs, ksc, wo, lg, lb, w1, b1, w2, b2):
            b, n, _ = x.shape
            h = shift_token(x)
            qkv = h @ wqkv
            q, k, v = jnp.split(qkv, 3, axis=-1)
            to_heads = lambda t: t.reshape(b, n, HEADS, DIM_HEAD).transpose(0, 2, 1, 3)
            q, k, v = (to_heads(q), to_heads(k), to_heads(v))
            q = l2norm(q) * qs
            k = l2norm(k) * ksc
            q, k = rotary_xpos(q, k)
            o = local_attention(q, k, v)
            o = o.transpose(0, 2, 1, 3).reshape(b, n, INNER)
            x = x + o @ wo
            h = shift_token(x)
            mu = h.mean(-1, keepdims=True)
            var = h.var(-1, keepdims=True)
            h = (h - mu) / jnp.sqrt(var + 1e-05) * lg + lb
            h = h @ w1 + b1
            a, g = jnp.split(h, 2, axis=-1)
            h = a * jax.nn.gelu(g, approximate=False)
            x = x + h @ w2 + b2
            return x
        for l in range(DEPTH):
            x = _layer(x, wqkv[l], q_scale[l], k_scale[l], wo[l], ln_g[l], ln_b[l], w1[l], b1[l], w2[l], b2[l])
        return x
    x = L0_attn_x
    xn = _layernorm(x, axis=-1)
    s = _L0_attn_ref(xn, L0_attn_W, L0_attn_b, L0_attn_ln_w, L0_attn_ln_b)
    g = _silu(_L0_ffn_ref(xn, L0_ffn_W_in, L0_ffn_b_in, L0_ffn_W_out))
    x = x + s * g
    xn = _layernorm(x, axis=-1)
    s = _L1_attn_ref(xn, L1_attn_Wq, L1_attn_Wk, L1_attn_Wv, L1_attn_conv_q, L1_attn_conv_k, L1_attn_conv_v, L1_attn_Wb, L1_attn_Wa, L1_attn_A_log, L1_attn_dt_bias, L1_attn_Wg, L1_attn_norm_w, L1_attn_Wo)
    g = _silu(_L1_ffn_ref(xn, L1_ffn_wqkv, L1_ffn_q_scale, L1_ffn_k_scale, L1_ffn_wo, L1_ffn_ln_g, L1_ffn_ln_b, L1_ffn_w1, L1_ffn_b1, L1_ffn_w2, L1_ffn_b2))
    x = x + s * g
    return x

_drawn_inputs = setup_inputs


def setup_inputs(seed=0):
    import zlib

    import numpy as np

    out = dict(_drawn_inputs(seed))
    spreads = {'L1_attn_norm_w': (1.0, 0.6),
     'L1_ffn_q_scale': (1.0, 0.6),
     'L1_ffn_k_scale': (1.0, 0.6),
     'L1_ffn_ln_g': (1.0, 0.6),
     'L1_ffn_ln_b': (0.0, 0.8),
     'L1_ffn_b1': (0.0, 0.8),
     'L1_ffn_b2': (0.0, 0.8)}
    factors = {'L0_attn_b': 8.0,
     'L0_attn_ln_w': 8.0,
     'L0_attn_ln_b': 8.0,
     'L1_attn_Wq': 3.911,
     'L1_attn_Wk': 3.931,
     'L1_attn_Wv': 3.937,
     'L1_attn_conv_q': 3.969,
     'L1_attn_conv_k': 3.938,
     'L1_attn_conv_v': 3.922,
     'L1_attn_Wb': 8.0,
     'L1_attn_Wa': 8.0,
     'L1_attn_A_log': 8.0,
     'L1_attn_dt_bias': 8.0,
     'L1_attn_Wg': 3.932,
     'L1_attn_Wo': 3.923,
     'L1_ffn_wqkv': 8.0,
     'L1_ffn_wo': 8.0,
     'L1_ffn_w1': 8.0,
     'L1_ffn_w2': 8.0}
    for name, (base, spread) in spreads.items():
        noise = np.random.default_rng([zlib.crc32(name.encode()), seed]).standard_normal(out[name].shape)
        drawn = base * np.exp(spread * noise) if base else spread * noise
        out[name] = jnp.asarray(drawn.astype(out[name].dtype))
    for name, factor in factors.items():
        out[name] = (out[name] * factor).astype(out[name].dtype)
    return out
```

```python
from contextlib import ExitStack

import numpy as np

import concourse.bass as bass
from concourse import mybir

F32 = mybir.dt.float32
BF16 = mybir.dt.bfloat16
U32 = mybir.dt.uint32
I32 = mybir.dt.int32
ALU = mybir.AluOpType
ACT = mybir.ActivationFunctionType
AX = mybir.AxisListType

P = 128
B, T, D = 16, 256, 128
NT = B * T // P
GT = 4
GW = GT * P
NG = NT // GT
SG = GW // T
EPS = 1e-5

TREES, FAN, DEPTH = 4, 4, 5
TOP = 4
TOP_AT = [TREES * FAN * (FAN ** d - 1) // (FAN - 1) for d in range(TOP + 1)]
TOPW = TOP_AT[TOP]
TCH = -(-TOPW // P)
TLAST = TOPW - (TCH - 1) * P
PICK = TREES * FAN
ROW = 2 * FAN * D + FAN

NH, HD = 16, 8
TAPS = 4
PADT = T + TAPS - 1
CH = 16
NCH = T // CH

LAYERS, HEADS, DH, WIN = 2, 8, 64, 64
INNER = HEADS * DH
HID = 341
HCH = [(0, 128), (128, 128), (256, 85)]
MASKED = -1e30
SOFT = [1.0 / (2 * k + 1) for k in range(8)]

COLS = dict(b0=0, lnw=4, lnb=5, eps6=6, eps5=7, nw=8, lng=9, lnb1=11, b1a=13, b1g=19)
NCOL = 25


class Phase(ExitStack):

    def __init__(self, nc):
        super().__init__()
        self.nc, self.used = nc, []

    def semaphore(self, name):
        s = self.enter_context(self.nc.semaphore(name))
        self.used.append(s)
        return s

    def block(self):
        self.callback(self.zero)
        return self.enter_context(self.nc.Block())

    def zero(self):
        with self.nc.Block() as block:
            @block.sync
            def _(sp):
                for s in self.used:
                    sp.sem_clear(s)


class Step:

    def __init__(self, ctx, nc, name, per=1):
        self.sem, self.per = ctx.semaphore(name), per

    def after(self, u, k=None):
        return u * self.per + (self.per if k is None else k)


class Chain:

    def __init__(self, ctx, nc, eng, name, per):
        self.sem, self.per, self.eng, self.n = ctx.semaphore(name), per, eng, 0
        self.unit = 0

    def begin(self, u):
        self.unit, self.n = u, 0

    def mark(self, ins):
        self.n += 1
        ins.then_inc(self.sem, 1)
        return self.n

    def wait(self, n):
        self.eng.wait_ge(self.sem, self.unit * self.per + n)

    def link(self, ins):
        self.wait(self.mark(ins))

    def end(self):
        assert self.n == self.per, (self.n, self.per)


def skewed(eng, count, steps):
    lag = max(l for _, l in steps)
    first = lag + 2 + (lag % 2)
    last = count - (count % 2)

    def round_(t, par, whole):
        for fn, l in steps:
            if whole or 0 <= t - l < count:
                fn(t - l, (par - l) % 2)

    for t in range(min(first, last)):
        round_(t, t % 2, False)
    if last > first:
        with eng.Fori(first // 2, last // 2) as i:
            for par in (0, 1):
                round_(i * 2 + par, par, True)
    for t in range(max(first, last) if last <= first else last, count + lag):
        round_(t, t % 2, False)


def known(u, least):
    return not isinstance(u, int) or u >= least


def flat(ap):
    return ap.rearrange("p a b -> p (a b)")


def load_phase(nc, m, inp):
    with Phase(nc) as ctx:
        loaded = ctx.semaphore("loaded")
        block = ctx.block()
        pairs = [(m[name][:], inp[name]) for name in m["loads"]]
        half = len(pairs) // 2

        @block.sync
        def _(sp):
            for dst, src in pairs[:half]:
                sp.dma_start(dst, src).then_inc(loaded, 16)
            sp.wait_ge(loaded, 16 * len(pairs))

        @block.scalar
        def _(act):
            for dst, src in pairs[half:]:
                act.dma_start(dst, src).then_inc(loaded, 16)
            act.wait_ge(loaded, 16 * len(pairs))


RSQRT_OPS = 12


def rsqrt(dve, ch, out, v, add, half, bits, a, floor=None):
    if floor is None:
        ch.link(dve.tensor_scalar(half, v, add, 0.5, ALU.add, ALU.mult))
    else:
        ch.link(dve.tensor_scalar(half, v, floor, 0.5, ALU.max, ALU.mult))
    ch.link(dve.tensor_scalar(bits, half.bitcast(I32), 1, None, ALU.logical_shift_right))
    ch.link(dve.tensor_scalar(out.bitcast(I32), bits, -1.0, float(0x5F3759DF - 2 ** 31 - 2 ** 22), ALU.mult, ALU.add))
    for _ in range(3):
        ch.link(dve.tensor_tensor(a, out, out, ALU.mult))
        ch.link(dve.tensor_tensor(a, a, half, ALU.mult))
        ch.link(dve.scalar_tensor_tensor(out, a, 1.5, out, ALU.subtract, ALU.mult))


class RowNorm:

    def __init__(self, ctx, sb, name, tiles):
        self.tiles, self.held = tiles, ctx.semaphore(name + "_held")
        self.stats, self.mv = sb(name + "_stats", [P, tiles, 6]), sb(name + "_mv", [P, tiles, 2])
        self.half, self.a, self.rstd = (sb(name + k, [P, tiles]) for k in ("_half", "_a", "_rstd"))
        self.bits = sb(name + "_bits", [P, tiles], I32)
        self.links = 2 * tiles + RSQRT_OPS

    def __call__(self, dve, ch, x, out, ready):
        for j in range(self.tiles):
            n = ch.mark(dve.bn_stats(self.stats[:, j, :], x(j)))
        ch.wait(n)
        dve.sem_inc(self.held)
        for j in range(self.tiles):
            n = ch.mark(dve.bn_aggr(self.mv[:, j, :], self.stats[:, j, :]))
        ch.wait(n)
        rsqrt(dve, ch, self.rstd[:], self.mv[:, :, 1], EPS, self.half[:], self.bits[:], self.a[:])
        for j in range(self.tiles):
            ins = dve.tensor_scalar(out(j), x(j), self.mv[:, j, 0:1], self.rstd[:, j:j + 1], ALU.subtract, ALU.mult)
        ins.then_inc(ready.sem, 1)


def gates_phase(nc, m):
    with Phase(nc) as ctx:
        sb = lambda n, s, d=F32: ctx.enter_context(nc.sbuf_tensor(n, s, d))
        ps = lambda n, s, d=F32: ctx.enter_context(nc.psum_tensor(n, s, d))
        st = lambda n, per=1: Step(ctx, nc, n, per)
        xnorm, cnorm = RowNorm(ctx, sb, "ga_x", GT), RowNorm(ctx, sb, "ga_c", GT)
        xn = sb("ga_xn", [P, 2, GT, D])
        xT = sb("ga_xT", [P, 2, GW])
        gate = sb("ga_gate", [P, 2, 3, GW])
        ogate = sb("ga_ogate", [P, 2, GT, D])
        iz, c = sb("ga_iz", [P, 2, GW]), sb("ga_cstate", [P, 2, GW])
        n_, nw, th = (sb("ga_" + k, [P, 2, GT, D]) for k in ("n", "nw", "th"))
        turn_ps = [ps(f"ga_turn{k}", [P, GW]) for k in (0, 1)]
        gate_ps = [ps(f"ga_gps{k}", [P, GW]) for k in range(4)]
        c_ps = [ps(f"ga_cps{k}", [P, GW]) for k in (0, 1)]
        xn_ready, xT_turned, xT_ready = st("xn_ready"), st("xT_turned"), st("xT_ready")
        gates_summed, gates_ready = st("gates_summed", 4), st("gates_ready", 4)
        c_ready, c_turned, normed = st("c_ready"), st("c_turned"), st("c_normed")
        affine, th_ready, s_ready, xn_saved = st("c_affine"), st("th_ready"), st("s_ready"), st("xn_saved")
        block = ctx.block()
        col = lambda k, i=0: m["cols"][:, COLS[k] + i:COLS[k] + i + 1]
        WHICH = [0, 1, 3, 2]

        @block.vector
        def _(dve):
            chf = Chain(ctx, nc, dve, "ga_dve_norm", xnorm.links)
            chb = Chain(ctx, nc, dve, "ga_dve_scan", 2 + cnorm.links)

            def norm(g, par):
                chf.begin(g)
                if known(g, 2):
                    dve.wait_ge(xT_turned.sem, xT_turned.after(g - 2))
                    dve.wait_ge(xn_saved.sem, xn_saved.after(g - 2))
                xnorm(dve, chf, lambda j: m["x_tok"][:, bass.ds(g * GT + j, 1), :].rearrange("p a d -> p (a d)"),
                      lambda j: xn[:, par, j, :], xn_ready)
                chf.end()

            def scan(g, par):
                chb.begin(g)
                dve.wait_ge(gates_ready.sem, gates_ready.after(g, 3))
                chb.link(dve.tensor_tensor(iz[:, par, :], gate[:, par, 1, :], gate[:, par, 2, :], ALU.mult))
                if known(g, 2):
                    dve.wait_ge(c_turned.sem, c_turned.after(g - 2))
                for s in range(SG):
                    w = slice(s * T, (s + 1) * T)
                    ins = dve.tensor_tensor_scan(c[:, par, w], gate[:, par, 0, w], iz[:, par, w], 0.0,
                                                 ALU.mult, ALU.add)
                ins.then_inc(c_ready.sem, 1)
                dve.wait_ge(c_turned.sem, c_turned.after(g))
                if known(g, 2):
                    dve.wait_ge(affine.sem, affine.after(g - 2))
                cnorm(dve, chb, lambda j: c_ps[par][:, j * P:(j + 1) * P], lambda j: n_[:, par, j, :], normed)
                dve.wait_ge(th_ready.sem, th_ready.after(g))
                dve.wait_ge(gates_ready.sem, gates_ready.after(g))
                chb.link(dve.tensor_tensor(m["s_tok"][:, bass.ds(g * GT, GT), :], ogate[:, par, :, :], th[:, par, :, :], ALU.mult))
                dve.nop().then_inc(s_ready.sem, 1)
                chb.end()

            skewed(dve, NG, [(norm, 0), (scan, 1)])

        @block.gpsimd
        def _(pool):
            chp = Chain(ctx, nc, pool, "ga_pool", 1)
            rows = lambda k: m[k][:].unsqueeze(1).broadcast_to([P, GT, D])

            def scale(g, par):
                chp.begin(g)
                pool.wait_ge(normed.sem, normed.after(g))
                if known(g, 2):
                    pool.wait_ge(th_ready.sem, th_ready.after(g - 2))
                chp.link(pool.tensor_tensor(nw[:, par, :, :], n_[:, par, :, :], rows("lnw0"), ALU.mult))
                pool.tensor_tensor(nw[:, par, :, :], nw[:, par, :, :], rows("lnb0"), ALU.add).then_inc(affine.sem, 1)

            skewed(pool, NG, [(scale, 0)])

        @block.tensor
        def _(pe):
            def front(g, par):
                pe.wait_ge(xn_ready.sem, xn_ready.after(g))
                if known(g, 2):
                    pe.wait_ge(xT_ready.sem, xT_ready.after(g - 2))
                for j in range(GT):
                    ins = pe.transpose(turn_ps[par][:, j * P:(j + 1) * P], xn[:, par, j, :], m["ident"][:])
                ins.then_inc(xT_turned.sem, 1)
                pe.wait_ge(xT_ready.sem, xT_ready.after(g))
                for k, q in enumerate(WHICH):
                    if known(g, 1):
                        pe.wait_ge(gates_ready.sem, gates_ready.after(g - 1, k + 1))
                    w = m["W0T"][:, q * P:(q + 1) * P]
                    if q != 2:
                        ins = pe.matmul(gate_ps[k][:], w, xT[:, par, :], start=True, stop=True)
                    else:
                        for j in range(GT):
                            at = slice(j * P, (j + 1) * P)
                            pe.matmul(gate_ps[k][:, at], m["ones"][0:1, :], m["bo0"][0:1, :], start=True, stop=False)
                            ins = pe.matmul(gate_ps[k][:, at], xT[:, par, at], w, start=False, stop=True)
                    ins.then_inc(gates_summed.sem, 1)

            def back(g, par):
                pe.wait_ge(c_ready.sem, c_ready.after(g))
                if known(g, 2):
                    pe.wait_ge(normed.sem, normed.after(g - 2))
                for j in range(GT):
                    ins = pe.transpose(c_ps[par][:, j * P:(j + 1) * P], c[:, par, j * P:(j + 1) * P], m["ident"][:])
                ins.then_inc(c_turned.sem, 1)

            skewed(pe, NG, [(front, 0), (back, 1)])

        @block.scalar
        def _(act):
            def front(g, par):
                act.wait_ge(xT_turned.sem, xT_turned.after(g))
                if known(g, 2):
                    act.wait_ge(gates_summed.sem, gates_summed.after(g - 2))
                act.copy(xT[:, par, :], turn_ps[par][:]).then_inc(xT_ready.sem, 1)
                act.wait_ge(xn_ready.sem, xn_ready.after(g))
                act.copy(m["xn_tok"][:, bass.ds(g * GT, GT), :], xn[:, par, :, :]).then_inc(xn_saved.sem, 1)
                for k, q in enumerate(WHICH):
                    act.wait_ge(gates_summed.sem, gates_summed.after(g, k + 1))
                    if known(g, 2):
                        act.wait_ge(s_ready.sem, s_ready.after(g - 2))
                    if q != 2:
                        ins = act.activation(gate[:, par, k, :], gate_ps[k][:], ACT.Tanh if q == 3 else ACT.Sigmoid, bias=col("b0", q))
                    else:
                        ins = act.activation(flat(ogate[:, par, :, :]), gate_ps[k][:], ACT.Sigmoid)
                    ins.then_inc(gates_ready.sem, 1)

            def back(g, par):
                act.wait_ge(affine.sem, affine.after(g))
                if known(g, 2):
                    act.wait_ge(s_ready.sem, s_ready.after(g - 2))
                act.activation(th[:, par, :, :], nw[:, par, :, :], ACT.Tanh).then_inc(th_ready.sem, 1)

            skewed(act, NG, [(front, 0), (back, 1)])


def choose(dve, ch, pick, t1, t2, wt, mx, mw, rel, base, last=None):
    tree_f = lambda a: a.rearrange("p (t f) -> p t f", f=FAN)
    ch.link(dve.tensor_reduce(mx, tree_f(pick), AX.X, ALU.max))
    ch.link(dve.tensor_tensor(tree_f(t1), tree_f(pick), mx.unsqueeze(2).broadcast_to([P, TREES, FAN]), ALU.is_equal))
    ch.link(dve.tensor_tensor(t2, t1, wt, ALU.mult))
    ch.link(dve.tensor_reduce(mw, tree_f(t2), AX.X, ALU.max))
    ins = dve.tensor_tensor(rel, base, mw, ALU.subtract)
    if last is None:
        ch.link(ins)
    return ins


def tree_top_phase(nc, m):
    with Phase(nc) as ctx:
        sb = lambda n, s, d=F32: ctx.enter_context(nc.sbuf_tensor(n, s, d))
        ps = lambda n, s, d=F32: ctx.enter_context(nc.psum_tensor(n, s, d))
        st = lambda n, per=1: Step(ctx, nc, n, per)
        xT, xn = sb("tt_xT", [P, 2, P]), sb("tt_xn", [P, 2, D])
        A, M = sb("tt_A", [P, 2, TOPW]), sb("tt_M", [P, 2, TOPW])
        MT = sb("tt_MT", [P, 2, TCH, P])
        mask = sb("tt_mask", [P, TREES * FAN ** (TOP - 1)])
        pick, t1, t2 = (sb("tt_" + k, [P, PICK]) for k in ("pick", "t1", "t2"))
        mx, mw, rel, base = (sb("tt_" + k, [P, TREES]) for k in ("mx", "mw", "rel", "base"))
        log_ps = [ps(f"tt_log{k}", [P, 512]) for k in range(3)]
        turn_ps = ps("tt_turn", [P, 3, 512])
        sum_ps = ps("tt_sum", [P, 512])
        x_ps = ps("tt_x", [P, 512])
        tile_in, x_turned, xT_ready = st("tile_in"), st("tt_x_turned"), st("tt_xT_ready")
        logits, acts, picked = st("logits"), st("acts_ready"), st("masked_ready")
        turned, MT_ready, summed, saved = st("masked_turned"), st("MT_ready"), st("top_summed"), st("top_saved")
        block = ctx.block()
        W = [(k * 512, min(512, TOPW - k * 512)) for k in range(3)]

        @block.tensor
        def _(pe):
            def front(t, par):
                pe.wait_ge(tile_in.sem, tile_in.after(t))
                if known(t, 1):
                    pe.wait_ge(xT_ready.sem, xT_ready.after(t - 1))
                pe.transpose(x_ps[:, 0:P], xn[:, par, :], m["ident"][:]).then_inc(x_turned.sem, 1)
                pe.wait_ge(xT_ready.sem, xT_ready.after(t))
                if known(t, 1):
                    pe.wait_ge(acts.sem, acts.after(t - 1))
                for k, (at, w) in enumerate(W):
                    pe.matmul(log_ps[k][:, 0:w], m["ones"][0:1, :], m["top_b"][0:1, at:at + w], start=True, stop=False)
                    ins = pe.matmul(log_ps[k][:, 0:w], xT[:, par, :], m["top_in"][:, at:at + w], start=False, stop=True)
                ins.then_inc(logits.sem, 1)

            def back(t, par):
                pe.wait_ge(picked.sem, picked.after(t))
                if known(t, 1):
                    pe.wait_ge(MT_ready.sem, MT_ready.after(t - 1))
                for k in range(TCH):
                    w = P if k < TCH - 1 else TLAST
                    ins = pe.transpose(turn_ps[0:w, k // 4, (k % 4) * P:(k % 4 + 1) * P],
                                       M[:, par, k * P:k * P + w], m["ident"][:])
                ins.then_inc(turned.sem, 1)
                pe.wait_ge(MT_ready.sem, MT_ready.after(t))
                if known(t, 1):
                    pe.wait_ge(saved.sem, saved.after(t - 1))
                for k in range(TCH):
                    w = P if k < TCH - 1 else TLAST
                    ins = pe.matmul(sum_ps[:, 0:D], MT[0:w, par, k, :], m["top_out"][0:w, k, :],
                                    start=(k == 0), stop=(k == TCH - 1))
                ins.then_inc(summed.sem, 1)

            skewed(pe, NT, [(front, 0), (back, 1)])

        @block.scalar
        def _(act):
            def front(t, par):
                if known(t, 2):
                    act.wait_ge(x_turned.sem, x_turned.after(t - 2))
                act.copy(xn[:, par, :], m["xn_tok"][:, bass.ds(t, 1), :].rearrange("p a d -> p (a d)")).then_inc(tile_in.sem, 1)
                act.wait_ge(x_turned.sem, x_turned.after(t))
                if known(t, 2):
                    act.wait_ge(logits.sem, logits.after(t - 2))
                act.copy(xT[:, par, :], x_ps[:, 0:P]).then_inc(xT_ready.sem, 1)
                act.wait_ge(logits.sem, logits.after(t))
                if known(t, 2):
                    act.wait_ge(picked.sem, picked.after(t - 2))
                for k, (at, w) in enumerate(W):
                    ins = act.activation(A[:, par, at:at + w], log_ps[k][:, 0:w], ACT.Gelu)
                ins.then_inc(acts.sem, 1)

            def back(t, par):
                act.wait_ge(turned.sem, turned.after(t))
                if known(t, 2):
                    act.wait_ge(summed.sem, summed.after(t - 2))
                full = (TCH - 1) // 4 * 4
                act.copy(MT[:, par, 0:full, :].rearrange("p k c -> p (k c)"), turn_ps[:, 0:full // 4, :].rearrange("p a c -> p (a c)"))
                rest = TCH - 1 - full
                act.copy(MT[:, par, full:TCH - 1, :].rearrange("p k c -> p (k c)"), turn_ps[:, full // 4, 0:rest * P])
                act.copy(MT[0:TLAST, par, TCH - 1, :], turn_ps[0:TLAST, full // 4, rest * P:(rest + 1) * P]).then_inc(MT_ready.sem, 1)
                act.wait_ge(summed.sem, summed.after(t))
                act.copy(m["f_tok"][:, bass.ds(t, 1), :].rearrange("p a d -> p (a d)"), sum_ps[:, 0:D]).then_inc(saved.sem, 1)

            skewed(act, NT, [(front, 0), (back, 1)])

        @block.vector
        def _(dve):
            ch = Chain(ctx, nc, dve, "tt_dve", TOP * 5 + (TOP - 1) * 4)

            def select(t, par):
                ch.begin(t)
                dve.wait_ge(acts.sem, acts.after(t))
                if known(t, 2):
                    dve.wait_ge(turned.sem, turned.after(t - 2))
                Af, Mf = A[:, par, :], M[:, par, :]
                dve.tensor_copy(Mf[:, 0:PICK], Af[:, 0:PICK])
                for d in range(TOP):
                    n = FAN ** d
                    at, end = TOP_AT[d], TOP_AT[d + 1]
                    if d:
                        mk = mask[:, 0:TREES * n]
                        ch.link(dve.tensor_tensor(mk.rearrange("p (t n) -> p t n", n=n),
                                                  m["iota"][:, 0:n].unsqueeze(1).broadcast_to([P, TREES, n]),
                                                  rel[:].unsqueeze(2).broadcast_to([P, TREES, n]), ALU.is_equal))
                        ch.link(dve.tensor_tensor(Mf[:, at:end].rearrange("p (a f) -> p a f", f=FAN),
                                                  Af[:, at:end].rearrange("p (a f) -> p a f", f=FAN),
                                                  mk.unsqueeze(2).broadcast_to([P, TREES * n, FAN]), ALU.mult))
                        ch.link(dve.tensor_reduce(pick[:].rearrange("p (t f) -> p t f", f=FAN),
                                                  Mf[:, at:end].rearrange("p (t n f) -> p t f n", t=TREES, f=FAN),
                                                  AX.X, ALU.add))
                        chosen = pick[:]
                        ch.link(dve.tensor_scalar(base[:], rel[:], float(FAN), float(FAN), ALU.mult, ALU.add))
                        choose(dve, ch, chosen, t1[:], t2[:], m["first"][:], mx[:], mw[:], rel[:], base[:])
                    else:
                        choose(dve, ch, Af[:, 0:PICK], t1[:], t2[:], m["first"][:], mx[:], mw[:], rel[:], m["four"][:])
                dve.tensor_copy(m["rel_all"][:, bass.ds(t, 1), :].rearrange("p a d -> p (a d)"), rel[:]).then_inc(picked.sem, 1)
                dve.wait_ge(picked.sem, picked.after(t))
                ch.end()

            skewed(dve, NT, [(select, 0)])


def tree_deep_phase(nc, m, table4, table5):
    with Phase(nc) as ctx:
        sb = lambda n, s, d=F32: ctx.enter_context(nc.sbuf_tensor(n, s, d))
        st = lambda n, per=1: Step(ctx, nc, n, per)
        rows4, rows5 = sb("td_rows4", [P, 2, TREES, ROW]), sb("td_rows5", [P, 2, TREES, ROW])
        idx4, idx5 = sb("td_idx4", [P, 2, TREES], U32), sb("td_idx5", [P, 2, TREES], U32)
        xn = sb("td_xn", [P, 2, D])
        rel4 = sb("td_rel4", [P, 2, TREES])
        dot4, dot5, pick4, pick5, act4, act5 = (sb("td_" + k, [P, 2, PICK]) for k in
                                                ("dot4", "dot5", "pick4", "pick5", "act4", "act5"))
        mark = sb("td_mark", [P, 1])
        acc = sb("td_acc", [P, 2, TREES, D])
        t1, t2 = sb("td_t1", [P, PICK]), sb("td_t2", [P, PICK])
        mx, mw, rel, base = (sb("td_" + k, [P, TREES]) for k in ("mx", "mw", "rel", "base"))
        held = ctx.semaphore("td_held")
        got4 = [st(f"got4_{k}", 16 * TREES) for k in (0, 1)]
        got5 = [st(f"got5_{k}", 16 * TREES) for k in (0, 1)]
        idx4_ready, idx5_ready, xn_ready = st("idx4_ready"), st("idx5_ready"), st("td_xn_ready")
        pick4_ready, pick5_ready = st("pick4_ready"), st("pick5_ready")
        act4_ready, act5_ready = st("act4_ready"), st("act5_ready")
        used4, used5 = st("rows4_used"), st("rows5_used")
        block = ctx.block()

        @block.gpsimd
        def _(pool):
            def gather(rows, idx, table, got, idx_ready, used):
                def fn(t, par):
                    pool.wait_ge(idx_ready.sem, idx_ready.after(t))
                    if known(t, 2):
                        pool.wait_ge(used.sem, used.after(t - 2))
                    pool.sem_inc(held)
                    for p in range(TREES):
                        pool.indirect_dma_start(rows[:, par, p, :], None, table,
                                                bass.IndirectOffsetOnAxis(ap=idx[:, par, p:p + 1], axis=0)).then_inc(got[par].sem, 16)
                return fn
            skewed(pool, NT, [(gather(rows4, idx4, table4, got4, idx4_ready, used4), 0),
                              (gather(rows5, idx5, table5, got5, idx5_ready, used5), 1)])

        @block.scalar
        def _(act):
            def gelu(pick, out, pick_ready, act_ready, used):
                def fn(t, par):
                    act.wait_ge(pick_ready.sem, pick_ready.after(t))
                    if known(t, 2):
                        act.wait_ge(used.sem, used.after(t - 2))
                    act.activation(out[:, par, :], pick[:, par, :], ACT.Gelu).then_inc(act_ready.sem, 1)
                return fn

            def tile_in(t, par):
                if known(t, 2):
                    act.wait_ge(pick5_ready.sem, pick5_ready.after(t - 2))
                act.copy(xn[:, par, :], m["xn_tok"][:, bass.ds(t, 1), :].rearrange("p a d -> p (a d)")).then_inc(xn_ready.sem, 1)
            skewed(act, NT, [(gelu(pick4, act4, pick4_ready, act4_ready, used4), 1),
                             (gelu(pick5, act5, pick5_ready, act5_ready, used5), 2), (tile_in, 0)])

        @block.vector
        def _(dve):
            chi = Chain(ctx, nc, dve, "td_dve_index", 1)
            ch4 = Chain(ctx, nc, dve, "td_dve_level4", 2 + 5 + 4)
            ch5 = Chain(ctx, nc, dve, "td_dve_level5", 1 + 4)

            def index(t, par):
                chi.begin(t)
                chi.link(dve.tensor_copy(rel4[:, par, :], m["rel_all"][:, bass.ds(t, 1), :].rearrange("p a d -> p (a d)")))
                if known(t, 2):
                    dve.wait_ge(got4[par].sem, got4[par].per * (t - par) // 2 if isinstance(t, int) else (t - par) * (got4[par].per // 2))
                dve.tensor_tensor(idx4[:, par, :], rel4[:, par, :], m["base4"][:], ALU.add).then_inc(idx4_ready.sem, 1)

            def dots(ch, rows, dot, pick, got, pick_ready, t, par):
                dve.wait_ge(xn_ready.sem, xn_ready.after(t))
                dve.wait_ge(got[par].sem, (t - par) * (got[par].per // 2) + got[par].per)
                for p in range(TREES):
                    for f in range(FAN):
                        k = p * FAN + f
                        ins = dve.tensor_tensor_reduce(rows[:, par, p, f * D:(f + 1) * D], rows[:, par, p, f * D:(f + 1) * D], xn[:, par, :],
                                                       1.0, 0.0, ALU.mult, ALU.add, dot[:, par, k:k + 1])
                ch.link(ins)
                tf = lambda a: a[:, par, :].rearrange("p (t f) -> p t f", f=FAN)
                dve.tensor_tensor(tf(pick), tf(dot), rows[:, par, :, 2 * FAN * D:], ALU.add).then_inc(pick_ready.sem, 1)

            def dots4(t, par):
                ch4.begin(t)
                dots(ch4, rows4, dot4, pick4, got4, pick4_ready, t, par)

            def dots5(t, par):
                ch5.begin(t)
                dots(ch5, rows5, dot5, pick5, got5, pick5_ready, t, par)

            def spread(ch, rows, act, t, par, first):
                for f in range(FAN):
                    for p in range(TREES):
                        w = rows[:, par, p, (FAN + f) * D:(FAN + f + 1) * D]
                        a = act[:, par, p * FAN + f:p * FAN + f + 1]
                        if first and f == 0 and p == 0:
                            ins = dve.scalar_tensor_tensor(acc[:, par, p, :], w, a,
                                                           m["f_tok"][:, bass.ds(t, 1), :].rearrange("p a d -> p (a d)"), ALU.mult, ALU.add)
                        elif first and f == 0:
                            ins = dve.tensor_scalar(acc[:, par, p, :], w, a, None, ALU.mult)
                        else:
                            ins = dve.scalar_tensor_tensor(acc[:, par, p, :], w, a, acc[:, par, p, :], ALU.mult, ALU.add)
                    if f < FAN - 1:
                        ch.link(ins)
                return ins

            def choose5(t, par):
                ch4.unit = t
                dve.wait_ge(act4_ready.sem, act4_ready.after(t))
                ch4.link(dve.tensor_scalar(base[:], rel4[:, par, :], float(FAN), float(FAN), ALU.mult, ALU.add))
                choose(dve, ch4, act4[:, par, :], t1[:], t2[:], m["first"][:], mx[:], mw[:], rel[:], base[:])
                if known(t, 2):
                    dve.wait_ge(got5[par].sem, (t - par) * (got5[par].per // 2))
                dve.tensor_tensor(idx5[:, par, :], rel[:], m["base5"][:], ALU.add).then_inc(idx5_ready.sem, 1)
                ins = spread(ch4, rows4, act4, t, par, True)
                ch4.mark(ins)
                dve.wait_ge(ch4.sem, t * ch4.per + ch4.n)
                dve.tensor_copy(mark[:], act4[:, par, 0:1]).then_inc(used4.sem, 1)
                assert ch4.n == ch4.per, ch4.n

            def finish(t, par):
                ch5.unit = t
                dve.wait_ge(act5_ready.sem, act5_ready.after(t))
                ins = spread(ch5, rows5, act5, t, par, False)
                ch5.link(ins)
                dve.sem_inc(held)
                dve.tensor_reduce(m["f_tok"][:, bass.ds(t, 1), :].rearrange("p a d -> p (a d)"),
                                  acc[:, par, :, :].rearrange("p t d -> p d t"), AX.X, ALU.add).then_inc(used5.sem, 1)
                assert ch5.n == ch5.per, ch5.n

            skewed(dve, NT, [(index, 0), (dots4, 1), (dots5, 2), (choose5, 1), (finish, 2)])


def merge_phase(nc, m):
    with Phase(nc) as ctx:
        sb = lambda n, s, d=F32: ctx.enter_context(nc.sbuf_tensor(n, s, d))
        ps = lambda n, s, d=F32: ctx.enter_context(nc.psum_tensor(n, s, d))
        st = lambda n, per=1: Step(ctx, nc, n, per)
        rownorm = RowNorm(ctx, sb, "me_n", GT)
        g_, sg, x1, xn = (sb("me_" + k, [P, 2, GT, D]) for k in ("g", "sg", "x1", "xn"))
        turn_ps = [ps(f"me_turn{k}", [P, GW]) for k in (0, 1)]
        g_ready, xn_ready, x1_ready = st("me_g_ready"), st("me_xn_ready"), st("me_x1_ready")
        turned, stored, kept = st("me_turned"), st("me_xT_stored"), st("me_kept", 2)
        zeroed = st("pad_zeroed")
        block = ctx.block()
        grp = lambda name, g: m[name][:, bass.ds(g * GT, GT), :]

        @block.scalar
        def _(act):
            def front(g, par):
                if known(g, 2):
                    act.wait_ge(x1_ready.sem, x1_ready.after(g - 2))
                act.activation(g_[:, par, :, :], grp("f_tok", g), ACT.Silu).then_inc(g_ready.sem, 1)

            def back(g, par):
                act.wait_ge(turned.sem, turned.after(g))
                act.copy(m["xT_pad"][:, bass.ds(g * SG, SG), TAPS - 1:], turn_ps[par][:].rearrange("p (s t) -> p s t", t=T)).then_inc(stored.sem, 1)
            skewed(act, NG, [(front, 0), (back, 1)])

        @block.gpsimd
        def _(pool):
            pool.memset(m["xT_pad"][:, :, 0:TAPS - 1], 0.0).then_inc(zeroed.sem, 1)

            def keep(g, par):
                pool.wait_ge(x1_ready.sem, x1_ready.after(g))
                pool.tensor_copy(grp("x_tok", g), x1[:, par, :, :]).then_inc(kept.sem, 1)
                pool.wait_ge(xn_ready.sem, xn_ready.after(g))
                pool.tensor_copy(grp("xn_tok", g), xn[:, par, :, :]).then_inc(kept.sem, 1)
            skewed(pool, NG, [(keep, 0)])

        @block.tensor
        def _(pe):
            def turn(g, par):
                pe.wait_ge(xn_ready.sem, xn_ready.after(g))
                if known(g, 2):
                    pe.wait_ge(stored.sem, stored.after(g - 2))
                for j in range(GT):
                    ins = pe.transpose(turn_ps[par][:, j * P:(j + 1) * P], xn[:, par, j, :], m["ident"][:])
                ins.then_inc(turned.sem, 1)
            skewed(pe, NG, [(turn, 0)])

        @block.vector
        def _(dve):
            ch = Chain(ctx, nc, dve, "me_dve", 1 + rownorm.links)

            def fn(g, par):
                ch.begin(g)
                dve.wait_ge(g_ready.sem, g_ready.after(g))
                if known(g, 2):
                    dve.wait_ge(kept.sem, kept.after(g - 2))
                    dve.wait_ge(turned.sem, turned.after(g - 2))
                ch.link(dve.tensor_tensor(sg[:, par, :, :], g_[:, par, :, :], grp("s_tok", g), ALU.mult))
                dve.tensor_tensor(x1[:, par, :, :], sg[:, par, :, :], grp("x_tok", g), ALU.add).then_inc(x1_ready.sem, 1)
                dve.wait_ge(x1_ready.sem, x1_ready.after(g))
                rownorm(dve, ch, lambda j: x1[:, par, j, :], lambda j: xn[:, par, j, :], xn_ready)
                ch.end()
            skewed(dve, NG, [(fn, 0)])


def sized(ap):
    return ap.rearrange("p a d -> p (a d)")


def prepare_phase(nc, m):
    with Phase(nc) as ctx:
        sb = lambda n, s, d=F32: ctx.enter_context(nc.sbuf_tensor(n, s, d))
        ps = lambda n, s, d=F32: ctx.enter_context(nc.psum_tensor(n, s, d))
        st = lambda n, per=1: Step(ctx, nc, n, per)
        wj = {x: sb(f"pr_w{x}", [P, TAPS, P]) for x in "qkv"}
        sq, rt = (sb("pr_" + k, [P, 2, 2, GW]) for k in ("sq", "rt"))
        za, ab, e, beta, u, t, w, p, a, sp = (sb("pr_" + k, [P, GW]) for k in (
            "za", "ab", "e", "beta", "u", "t", "w", "p", "a", "sp"))
        neg = sb("pr_negA", [P, 2])
        bank = [ps(f"pr_ps{k}", [P, GW]) for k in range(8)]
        made = st("conv_weights")
        projected, silued = st("projected", 3), st("silued", 3)
        squared, summed, rooted, scaled = st("squared", 2), st("squares_summed", 2), st("rooted", 2), st("scaled", 2)
        z_ready, abs_ready, soft_exp, a_ready, betas, z_kept = st("z_ready"), st("abs_ready"), st("soft_exp"), st("a_ready"), st("beta_ready"), st("z_kept")
        sp_ready, ab_ready, decay_exp = st("softplus_ready"), st("ab_ready"), st("negA_exp")
        spread, a_kept, products = st("decays_spread", 3), st("a_kept"), st("products", 2)
        block = ctx.block()
        col = lambda k, i=0: m["cols"][:, COLS[k] + i:COLS[k] + i + 1]
        into = {"q": "qT", "k": "kT", "v": "bvT"}
        grp = lambda name, g: m[name][:, bass.ds(g * SG, SG), :]
        two = lambda ap: ap.rearrange("p (s t) -> p s t", t=T)

        @block.tensor
        def _(pe):
            pe.wait_ge(made.sem, 1)

            def project(g, par):
                for n, x in enumerate("qkv"):
                    if known(g, 2):
                        pe.wait_ge(silued.sem, silued.after(g - 2, n + 1))
                    for j in range(TAPS):
                        ins = pe.matmul(bank[3 * par + n][:], wj[x][:, j, :], m["xT_pad"][:, bass.ds(g * SG, SG), j:j + T],
                                        start=(j == 0), stop=(j == TAPS - 1))
                    ins.then_inc(projected.sem, 1)

            skewed(pe, NG, [(project, 0)])
            for which, bk in (("WaP", 6), ("WbP", 7)):
                for g in range(NG):
                    ins = pe.matmul(bank[bk][:], m[which][:, g, :], m["xT_pad"][:, g * SG:(g + 1) * SG, TAPS - 1:],
                                    start=(g == 0), stop=(g == NG - 1))
            ins.then_inc(z_ready.sem, 1)
            pe.wait_ge(silued.sem, silued.after(NG - 1))

            def norm(g, par):
                for n in range(2):
                    pe.wait_ge(squared.sem, squared.after(g, n + 1))
                    if known(g, 2):
                        pe.wait_ge(rooted.sem, rooted.after(g - 2, n + 1))
                    pe.matmul(bank[2 * par + n][:], m["head_mat"][:], sq[:, par, n, :], start=True, stop=True).then_inc(summed.sem, 1)

            skewed(pe, NG, [(norm, 0)])
            pe.wait_ge(rooted.sem, rooted.after(NG - 1))
            pe.wait_ge(z_kept.sem, 1)
            for g in range(NG):
                for n, x in enumerate((a, beta, ab)):
                    pe.wait_ge((a_ready, betas, ab_ready)[n].sem, 1)
                    if g >= 2:
                        if n == 0:
                            pe.wait_ge(a_kept.sem, g - 1)
                        else:
                            pe.wait_ge(products.sem, products.after(g - 2, n))
                    pe.matmul(bank[3 * (g % 2) + n][:], m["group_mat"][:, g, :], x[:], start=True, stop=True).then_inc(spread.sem, 1)

        @block.scalar
        def _(act):
            def silu(g, par):
                for n, x in enumerate("qkv"):
                    act.wait_ge(projected.sem, projected.after(g, n + 1))
                    act.activation(grp(into[x], g), two(bank[3 * par + n][:]), ACT.Silu).then_inc(silued.sem, 1)

            skewed(act, NG, [(silu, 0)])
            act.wait_ge(silued.sem, silued.after(NG - 1))

            def square(g, par):
                for n, x in enumerate("qk"):
                    if known(g, 2):
                        act.wait_ge(summed.sem, summed.after(g - 2, n + 1))
                    act.activation(two(sq[:, par, n, :]), grp(into[x], g), ACT.Square).then_inc(squared.sem, 1)

            def root(g, par):
                for n in range(2):
                    act.wait_ge(summed.sem, summed.after(g, n + 1))
                    if known(g, 2):
                        act.wait_ge(scaled.sem, scaled.after(g - 2, n + 1))
                    act.activation(rt[:, par, n, :], bank[2 * par + n][:], ACT.Sqrt, bias=col("eps6")).then_inc(rooted.sem, 1)

            skewed(act, NG, [(square, 0), (root, 1)])
            act.wait_ge(z_ready.sem, 1)
            act.activation(za[:], bank[6][:], ACT.Identity, bias=m["dt_compact"][:, 0:1])
            act.activation(beta[:], bank[7][:], ACT.Exp, scale=-1.0).then_inc(z_kept.sem, 1)
            act.wait_ge(z_kept.sem, 1)
            act.activation(t[:], za[:], ACT.Abs).then_inc(abs_ready.sem, 1)
            act.wait_ge(abs_ready.sem, 1)
            act.activation(e[:], t[:], ACT.Exp, scale=-1.0).then_inc(soft_exp.sem, 1)
            act.activation(neg[:, 0:1], m["dt_compact"][:, 1:2], ACT.Exp).then_inc(decay_exp.sem, 1)
            act.wait_ge(sp_ready.sem, 1)
            act.activation(a[:], sp[:], ACT.Exp, scale=neg[:, 1:2]).then_inc(a_ready.sem, 1)
            for g in range(NG):
                act.wait_ge(spread.sem, spread.after(g, 1))
                act.copy(grp("aT", g), two(bank[3 * (g % 2)][:])).then_inc(a_kept.sem, 1)

        @block.vector
        def _(dve):
            for x in "qkv":
                ins = dve.tensor_tensor(wj[x][:], m[f"W{x}T"][:].unsqueeze(1).broadcast_to([P, TAPS, P]), m[f"conv_{x}"][:], ALU.mult)
            ins.then_inc(made.sem, 1)
            chn = Chain(ctx, nc, dve, "pr_dve_norm", 2)
            cho = Chain(ctx, nc, dve, "pr_dve_once", 0)

            def scale(g, par):
                chn.begin(g)
                for n, x in enumerate("qk"):
                    dve.wait_ge(rooted.sem, rooted.after(g, n + 1))
                    chn.link(dve.reciprocal(rt[:, par, n, :], rt[:, par, n, :]))
                    dve.scalar_tensor_tensor(grp(into[x], g), grp(into[x], g), HD ** -0.5 if x == "q" else 1.0,
                                             two(rt[:, par, n, :]), ALU.mult, ALU.mult).then_inc(scaled.sem, 1)
                chn.end()

            skewed(dve, NG, [(scale, 0)])
            link = cho.link
            dve.wait_ge(z_kept.sem, 1)
            link(dve.tensor_scalar(beta[:], beta[:], 1.0, None, ALU.add))
            dve.reciprocal(beta[:], beta[:]).then_inc(betas.sem, 1)
            dve.wait_ge(betas.sem, 1)
            dve.wait_ge(soft_exp.sem, 1)
            link(dve.tensor_scalar(u[:], e[:], 2.0, None, ALU.add))
            link(dve.reciprocal(u[:], u[:]))
            link(dve.tensor_tensor(t[:], e[:], u[:], ALU.mult))
            link(dve.tensor_tensor(w[:], t[:], t[:], ALU.mult))
            link(dve.tensor_scalar(p[:], w[:], SOFT[-1], None, ALU.mult))
            for c in SOFT[-2:0:-1]:
                link(dve.scalar_tensor_tensor(p[:], p[:], c, w[:], ALU.add, ALU.mult))
            link(dve.scalar_tensor_tensor(p[:], p[:], 1.0, t[:], ALU.add, ALU.mult))
            link(dve.tensor_scalar(sp[:], za[:], 0.0, None, ALU.max))
            dve.wait_ge(decay_exp.sem, 1)
            link(dve.tensor_scalar(neg[:, 1:2], neg[:, 0:1], -1.0, None, ALU.mult))
            dve.scalar_tensor_tensor(sp[:], p[:], 2.0, sp[:], ALU.mult, ALU.add).then_inc(sp_ready.sem, 1)
            dve.wait_ge(a_ready.sem, 1)
            dve.tensor_tensor(ab[:], a[:], beta[:], ALU.mult).then_inc(ab_ready.sem, 1)
            dve.wait_ge(scaled.sem, scaled.after(NG - 1))
            for g in range(NG):
                dve.wait_ge(spread.sem, spread.after(g))
                dve.tensor_tensor(grp("bvT", g), grp("bvT", g), two(bank[3 * (g % 2) + 1][:]), ALU.mult).then_inc(products.sem, 1)
                dve.tensor_tensor(grp("kabT", g), grp("kT", g), two(bank[3 * (g % 2) + 2][:]), ALU.mult).then_inc(products.sem, 1)


def delta_phase(nc, m):
    with Phase(nc) as ctx:
        sb = lambda n, s, d=F32: ctx.enter_context(nc.sbuf_tensor(n, s, d))
        st = lambda n, per=1: Step(ctx, nc, n, per)
        wide = {x: sb(f"de_{x}", [P, 2, CH, B, HD]) for x in ("kab", "k", "q")}
        S = m["s1_tok"][:].rearrange("p n d -> p (n d)").rearrange("p (c t b k) -> p c t b k", c=2, t=CH, b=B)
        ac, bvc = sb("de_a", [P, 2, CH, B]), sb("de_bv", [P, 2, CH, B])
        decayed = sb("de_aS", [P, 2, B, HD])
        kS, outer = sb("de_kS", [P, B, HD]), sb("de_outer", [P, B, HD])
        pred, dv = sb("de_pred", [P, B]), sb("de_dv", [P, B])
        half = [[ctx.enter_context(nc.psum_tensor(f"de_ps{s}{k}", [P, 2, B, CH], F32)) for k in range(4)] for s in (0, 1)]
        ORDER = ("kab", "k", "q")
        spread, widened = st("keys_spread", 12), st("keys_widened", 12)
        small, S_ready, decayed_ready = st("a_bv_kept"), st("S_ready", CH), st("decayed_ready", CH)
        held = ctx.semaphore("de_held")
        weighed, o_ready, zero = st("S_weighed"), st("o_ready"), st("S_zero")
        block = ctx.block()
        src = {"kab": "kabT", "k": "kT", "q": "qT"}

        @block.tensor
        def _(pe):
            def fn(c, par):
                for n, x in enumerate(ORDER):
                    s = (3 * par + n) % 2
                    for k in range(4):
                        at = 4 * n + k - 8
                        if at >= 0:
                            pe.wait_ge(widened.sem, widened.after(c, at + 1))
                        elif known(c, 1):
                            pe.wait_ge(widened.sem, widened.after(c - 1, 12 + at + 1))
                        for d in (0, 1):
                            ins = pe.matmul(half[s][k][:, d, :, :], m["spread_mat"][:, 2 * k + d, :],
                                            m[src[x]][:, :, bass.ds(c * CH, CH)], start=True, stop=True)
                        ins.then_inc(spread.sem, 1)
            skewed(pe, NCH, [(fn, 0)])

        @block.scalar
        def _(act):
            def fn(c, par):
                if known(c, 2):
                    act.wait_ge(S_ready.sem, S_ready.after(c - 2))
                    act.wait_ge(decayed_ready.sem, decayed_ready.after(c - 2))
                for t, name in ((ac, "aT"), (bvc, "bvT")):
                    ins = act.copy(t[:, par, :, :], m[name][:, :, bass.ds(c * CH, CH)].rearrange("p b t -> p t b"))
                ins.then_inc(small.sem, 1)
                for n, x in enumerate(ORDER):
                    s = (3 * par + n) % 2
                    if n == 2 and known(c, 2):
                        act.wait_ge(o_ready.sem, o_ready.after(c - 2))
                    for k in range(4):
                        act.wait_ge(spread.sem, spread.after(c, 4 * n + k + 1))
                        act.copy(wide[x][:, par, :, :, 2 * k:2 * k + 2],
                                 half[s][k][:].rearrange("p d b t -> p t b d")).then_inc(widened.sem, 1)
            skewed(act, NCH, [(fn, 0)])

        @block.gpsimd
        def _(pool):
            pool.memset(S[:, 1, CH - 1, :, :], 0.0).then_inc(zero.sem, 1)
            pool.wait_ge(zero.sem, 1)

            def fn(c, par):
                pool.wait_ge(small.sem, small.after(c))
                for s in range(CH):
                    prev = S[:, par, s - 1, :, :] if s else S[:, 1 - par, CH - 1, :, :]
                    if s:
                        pool.wait_ge(S_ready.sem, S_ready.after(c, s))
                    elif known(c, 1):
                        pool.wait_ge(S_ready.sem, S_ready.after(c - 1))
                    pool.tensor_tensor(decayed[:, s % 2, :, :], prev, ac[:, par, s, :].unsqueeze(2).broadcast_to([P, B, HD]),
                                       ALU.mult).then_inc(decayed_ready.sem, 1)
                    if s:
                        if s == 1:
                            pool.wait_ge(widened.sem, widened.after(c))
                        q = wide["q"][:, par, s - 1, :, :]
                        pool.tensor_tensor(q, q, prev, ALU.mult)
                pool.wait_ge(S_ready.sem, S_ready.after(c))
                q = wide["q"][:, par, CH - 1, :, :]
                pool.tensor_tensor(q, q, S[:, par, CH - 1, :, :], ALU.mult).then_inc(weighed.sem, 1)
            skewed(pool, NCH, [(fn, 0)])

        @block.vector
        def _(dve):
            ch = Chain(ctx, nc, dve, "de_dve", 4 * CH)
            dve.wait_ge(zero.sem, 1)

            def steps(c, par):
                ch.begin(c)
                dve.wait_ge(small.sem, small.after(c))
                dve.wait_ge(widened.sem, widened.after(c, 8))
                for s in range(CH):
                    prev = S[:, par, s - 1, :, :] if s else S[:, 1 - par, CH - 1, :, :]
                    ch.link(dve.tensor_tensor(kS[:], prev, wide["kab"][:, par, s, :, :], ALU.mult))
                    ch.link(dve.tensor_reduce(pred[:], kS[:], AX.X, ALU.add))
                    ch.link(dve.tensor_tensor(dv[:], bvc[:, par, s, :], pred[:], ALU.subtract))
                    ch.link(dve.tensor_tensor(outer[:], wide["k"][:, par, s, :, :], dv[:].unsqueeze(2).broadcast_to([P, B, HD]), ALU.mult))
                    dve.wait_ge(decayed_ready.sem, decayed_ready.after(c, s + 1))
                    if s == 0 and known(c, 2):
                        dve.wait_ge(weighed.sem, weighed.after(c - 2))
                    dve.tensor_tensor(S[:, par, s, :, :], decayed[:, s % 2, :, :], outer[:], ALU.add).then_inc(S_ready.sem, 1)
                    dve.wait_ge(S_ready.sem, S_ready.after(c, s + 1))
                ch.end()

            def output(c, par):
                dve.wait_ge(weighed.sem, weighed.after(c))
                dve.sem_inc(held)
                dve.tensor_reduce(m["kabT"][:, :, bass.ds(c * CH, CH)].rearrange("p b t -> p t b"),
                                  wide["q"][:, par, :, :, :], AX.X, ALU.add).then_inc(o_ready.sem, 1)

            skewed(dve, NCH, [(steps, 0), (output, 1)])


def delta_out_phase(nc, m):
    with Phase(nc) as ctx:
        sb = lambda n, s, d=F32: ctx.enter_context(nc.sbuf_tensor(n, s, d))
        ps = lambda n, s, d=F32: ctx.enter_context(nc.psum_tensor(n, s, d))
        st = lambda n, per=1: Step(ctx, nc, n, per)
        sq, rt, ri, sg, u = (sb("do_" + k, [P, 2, GW]) for k in ("sq", "rt", "ri", "sg", "u"))
        mean_ps, gate_ps, out_ps = ([ps(f"do_{n}{k}", [P, GW]) for k in (0, 1)] for n in ("mean", "gate", "out"))
        squared, summed, rooted, normed = st("do_squared"), st("do_summed"), st("do_rooted"), st("do_normed")
        gated, silued, u_ready, multiplied, kept = st("do_gated"), st("do_silued"), st("do_u_ready"), st("do_multiplied"), st("do_kept")
        block = ctx.block()
        col = lambda k, i=0: m["cols"][:, COLS[k] + i:COLS[k] + i + 1]
        grp = lambda name, g: m[name][:, bass.ds(g * SG, SG), :]
        two = lambda ap: ap.rearrange("p (s t) -> p s t", t=T)

        @block.tensor
        def _(pe):
            def mean(g, par):
                pe.wait_ge(squared.sem, squared.after(g))
                if known(g, 2):
                    pe.wait_ge(rooted.sem, rooted.after(g - 2))
                pe.matmul(mean_ps[par][:], m["head_mean"][:], sq[:, par, :], start=True, stop=True).then_inc(summed.sem, 1)

            def gate(g, par):
                if known(g, 2):
                    pe.wait_ge(silued.sem, silued.after(g - 2))
                pe.matmul(gate_ps[par][:], m["WgT"][:], m["xT_pad"][:, bass.ds(g * SG, SG), TAPS - 1:], start=True, stop=True).then_inc(gated.sem, 1)

            def out(g, par):
                pe.wait_ge(u_ready.sem, u_ready.after(g))
                if known(g, 2):
                    pe.wait_ge(kept.sem, kept.after(g - 2))
                for j in range(GT):
                    at = slice(j * P, (j + 1) * P)
                    ins = pe.matmul(out_ps[par][:, at], u[:, par, at], m["WoT"][:], start=True, stop=True)
                ins.then_inc(multiplied.sem, 1)

            skewed(pe, NG, [(mean, 0)])
            skewed(pe, NG, [(gate, 0), (out, 1)])

        @block.scalar
        def _(act):
            def square(g, par):
                if known(g, 2):
                    act.wait_ge(summed.sem, summed.after(g - 2))
                act.activation(two(sq[:, par, :]), grp("kabT", g), ACT.Square).then_inc(squared.sem, 1)

            def root(g, par):
                act.wait_ge(summed.sem, summed.after(g))
                if known(g, 2):
                    act.wait_ge(normed.sem, normed.after(g - 2))
                act.activation(rt[:, par, :], mean_ps[par][:], ACT.Sqrt, bias=col("eps5")).then_inc(rooted.sem, 1)

            def silu(g, par):
                act.wait_ge(gated.sem, gated.after(g))
                if known(g, 2):
                    act.wait_ge(u_ready.sem, u_ready.after(g - 2))
                act.activation(sg[:, par, :], gate_ps[par][:], ACT.Silu).then_inc(silued.sem, 1)

            def keep(g, par):
                act.wait_ge(multiplied.sem, multiplied.after(g))
                act.copy(sized(m["s1_tok"][:, bass.ds(g * GT, GT), :]), out_ps[par][:]).then_inc(kept.sem, 1)

            skewed(act, NG, [(square, 0), (root, 1)])
            skewed(act, NG, [(silu, 0), (keep, 1)])

        @block.vector
        def _(dve):
            ch = Chain(ctx, nc, dve, "do_dve", 1)

            def norm(g, par):
                ch.begin(g)
                dve.wait_ge(rooted.sem, rooted.after(g))
                ch.link(dve.reciprocal(ri[:, par, :], rt[:, par, :]))
                dve.tensor_tensor(grp("kabT", g), grp("kabT", g), two(ri[:, par, :]), ALU.mult).then_inc(normed.sem, 1)

            def product(g, par):
                dve.wait_ge(silued.sem, silued.after(g))
                if known(g, 2):
                    dve.wait_ge(multiplied.sem, multiplied.after(g - 2))
                dve.scalar_tensor_tensor(two(u[:, par, :]), grp("kabT", g), col("nw"), two(sg[:, par, :]), ALU.mult, ALU.mult).then_inc(u_ready.sem, 1)

            skewed(dve, NG, [(norm, 0)])
            dve.wait_ge(normed.sem, normed.after(NG - 1))
            skewed(dve, NG, [(product, 0)])


class Region:

    def __init__(self, ctx, nc, name, fills):
        self.fills = fills
        self.filled, self.drained = Step(ctx, nc, name + "_filled", fills), Step(ctx, nc, name + "_drained", fills)

    def free(self, pe, u, k):
        if k or known(u, 1):
            pe.wait_ge(self.drained.sem, self.drained.after(u, k) if k else self.drained.after(u - 1))

    def full(self, eng, u, k):
        eng.wait_ge(self.filled.sem, self.filled.after(u, k + 1))


def local_phase(nc, m, layer):
    L = layer
    with Phase(nc) as ctx:
        sb = lambda n, s, d=F32: ctx.enter_context(nc.sbuf_tensor(f"lo{L}_{n}", s, d))
        ps = lambda n, s, d=F32: ctx.enter_context(nc.psum_tensor(f"lo{L}_{n}", s, d))
        st = lambda n, per=1: Step(ctx, nc, f"lo{L}_{n}", per)
        HALF = HEADS // 2
        tab = sb("tab", [P, 2, 2, 2, DH])
        mask16, ident16 = sb("mask16", [P, 2, T], BF16), sb("ident16", [P, P], BF16)
        y = sb("y", [P, 2, 2, D])
        hT = sb("hT", [P, 2, T])
        sq = sb("sq", [P, 2, 2 * INNER])
        ss, half, bits, aa, rn = sb("ss", [P, 2, 2 * HEADS]), sb("half", [P, 2 * HEADS]), sb("bits", [P, 2 * HEADS], I32), sb("aa", [P, 2 * HEADS]), sb("rn", [P, 2, 2 * HEADS])
        c1, c2 = sb("c1", [P, 2, 2 * INNER]), sb("c2", [P, 2, 2 * INNER])
        V = sb("V", [P, 2, 2, INNER])
        qT, kT = sb("qT", [P, 2, HEADS // 2, T]), sb("kT", [P, 2, HEADS // 2, T])
        prob = sb("prob", [P, 2, HALF, T])
        nmx, sums, rsum = sb("nmx", [P, 2, HALF]), sb("sums", [P, 2, HEADS]), sb("rsum", [P, HEADS])
        pT = sb("pT", [P, 2, 2, HALF, P])
        o, oT = sb("o", [P, INNER]), sb("oT", [P, INNER])
        y1 = sb("y1", [P, 2, D])
        h2T, h2, hn, hnT = sb("h2T", [P, T]), sb("h2", [P, 2, D]), sb("hn", [P, 2, D]), sb("hnT", [P, T])
        gg, u = sb("gg", [P, 3, T]), sb("u", [P, 3, T])
        rownorm = RowNorm(ctx, sb, "rows", 2)
        qkv_ps = ps("qkv", [P, 3, 512])
        ft_ps = ps("ft", [P, 512])
        s_ps = ps("s", [P, 2, 512])
        bt_ps = ps("bt", [P, 512])
        o_ps = ps("o_ps", [P, 512])
        qkv, ft, sc, bt, os_ = (Region(ctx, nc, f"lo{L}_{n}", k) for n, k in
                                (("qkv", 2), ("front_turn", 5), ("scores", 7), ("back_turn", 11), ("sums", 5)))
        consts = st("consts", 3)
        y_in, hT_ready, sq_ready, qv_kept = st("y_in"), st("hT_ready"), st("sq_ready", 2), st("v_kept", 2)
        parts, rot_ready, qkT_ready = st("rot_parts", 2), st("rot_ready", 2), st("qkT_ready", 4)
        mx_ready, prob_ready, pT_ready = st("mx_ready", 4), st("prob_ready", 4), st("pT_ready", 6)
        o_ready, oT_ready, y1_ready = st("o_ready", 2), st("oT_ready", 2), st("y1_ready", 2)
        h2T_ready, h2_ready, hn_ready, hnT_ready = st("h2T_ready"), st("h2_ready"), st("hn_ready"), st("hnT_ready")
        gg_ready, u_ready, y2_ready = st("gg_ready", 3), st("u_ready", 3), st("y2_ready")
        block = ctx.block()
        col = lambda k, i=0: m["cols"][:, COLS[k] + i:COLS[k] + i + 1]
        KEYS = [(0, P), (WIN, T)]
        BLOCKS = [[0], [0, 1]]
        NB = [0, 2]
        BT = {(0, 0, 0): 0, (0, 1, 0): 1, "o0": 2, (1, 0, 0): 3, (1, 0, 1): 4, (1, 1, 0): 5, (1, 1, 1): 6,
              "o1": 7, "y1": 8, "h2": 9, "hn": 10}
        PT = {(0, 0, 0): 0, (0, 1, 0): 1, (1, 0, 0): 2, (1, 0, 1): 3, (1, 1, 0): 4, (1, 1, 1): 5}

        @block.tensor
        def _(pe):
            pe.wait_ge(consts.sem, 3)

            def front(b, par):
                pe.wait_ge(y_in.sem, y_in.after(b))
                ft.free(pe, b, 0)
                for i in (0, 1):
                    ins = pe.transpose(ft_ps[:, i * P:(i + 1) * P], y[:, par, i, :], m["ident"][:])
                ins.then_inc(ft.filled.sem, 1)
                pe.wait_ge(hT_ready.sem, hT_ready.after(b))
                for i in (0, 1):
                    qkv.free(pe, b, i)
                    for n in range(3):
                        ins = pe.matmul(qkv_ps[:, n, :], hT[:, par, i * P:(i + 1) * P], m["wqkv"][:, L, n * INNER:(n + 1) * INNER], start=True, stop=True)
                    ins.then_inc(qkv.filled.sem, 1)
                    pe.wait_ge(rot_ready.sem, rot_ready.after(b, i + 1))
                    for w in (0, 1):
                        ft.free(pe, b, 1 + 2 * i + w)
                        for k in range(4):
                            ins = pe.transpose(ft_ps[:, k * P:(k + 1) * P], c1[:, i, w * INNER + k * P:w * INNER + (k + 1) * P], m["ident"][:])
                        ins.then_inc(ft.filled.sem, 1)

            def back(b, par):
                for i in (0, 1):
                    k0, k1 = KEYS[i]
                    W = k1 - k0
                    for hf in (0, 1):
                        if i == 0 and hf == 0:
                            pe.wait_ge(qkT_ready.sem, qkT_ready.after(b))
                        sc.free(pe, b, 2 * i + hf)
                        for n in range(HALF):
                            h = hf * HALF + n
                            r = slice(64 * (h % 2), 64 * (h % 2) + 64)
                            dst = s_ps[:, h % 2, (n // 2) * 256:(n // 2) * 256 + W]
                            pe.matmul(dst, ident16[:], mask16[:, i, k0:k1], start=True, stop=False)
                            ins = pe.matmul(dst, qT[r, par, h // 2, i * P:(i + 1) * P], kT[r, par, h // 2, k0:k1], start=False, stop=True)
                        ins.then_inc(sc.filled.sem, 1)
                    for hf in (0, 1):
                        pe.wait_ge(prob_ready.sem, prob_ready.after(b, 2 * i + hf + 1))
                        for blk in BLOCKS[i]:
                            bt.free(pe, b, BT[i, hf, blk])
                            for n in range(HALF):
                                ins = pe.transpose(bt_ps[:, n * P:(n + 1) * P], prob[:, hf, n, blk * P:(blk + 1) * P], m["ident"][:])
                            ins.then_inc(bt.filled.sem, 1)
                    os_.free(pe, b, 2 * i)
                    for hf in (0, 1):
                        pe.wait_ge(pT_ready.sem, pT_ready.after(b, PT[i, hf, BLOCKS[i][-1]] + 1))
                        for n in range(HALF):
                            h = hf * HALF + n
                            dst = o_ps[:, h * DH:(h + 1) * DH]
                            hd = slice(h * DH, (h + 1) * DH)
                            if i == 0:
                                ins = pe.matmul(dst, pT[:, hf, 0, n, :], V[:, par, 0, hd], start=True, stop=True)
                            else:
                                pe.matmul(dst, pT[WIN:, hf, 0, n, :], V[WIN:, par, 0, hd], start=True, stop=False)
                                ins = pe.matmul(dst, pT[:, hf, 1, n, :], V[:, par, 1, hd], start=False, stop=True)
                    ins.then_inc(os_.filled.sem, 1)
                    pe.wait_ge(o_ready.sem, o_ready.after(b, i + 1))
                    bt.free(pe, b, BT[f"o{i}"])
                    for k in range(4):
                        ins = pe.transpose(bt_ps[:, k * P:(k + 1) * P], o[:, k * P:(k + 1) * P], m["ident"][:])
                    ins.then_inc(bt.filled.sem, 1)
                    pe.wait_ge(oT_ready.sem, oT_ready.after(b, i + 1))
                    os_.free(pe, b, 2 * i + 1)
                    for k in range(4):
                        ins = pe.matmul(o_ps[:, 0:D], oT[:, k * P:(k + 1) * P], m["wo"][:, L, k, :], start=(k == 0), stop=(k == 3))
                    ins.then_inc(os_.filled.sem, 1)
                for name, ready, srcs in (("y1", y1_ready, [y1[:, 0, :], y1[:, 1, :]]),
                                          ("h2", h2T_ready, [h2T[:, 0:P], h2T[:, P:T]]),
                                          ("hn", hn_ready, [hn[:, 0, :], hn[:, 1, :]])):
                    pe.wait_ge(ready.sem, ready.after(b))
                    bt.free(pe, b, BT[name])
                    for i in (0, 1):
                        ins = pe.transpose(bt_ps[:, i * P:(i + 1) * P], srcs[i], m["ident"][:])
                    ins.then_inc(bt.filled.sem, 1)
                pe.wait_ge(hnT_ready.sem, hnT_ready.after(b))
                for k, (at, w) in enumerate(HCH):
                    sc.free(pe, b, 4 + k)
                    for side in (0, 1):
                        ins = pe.matmul(s_ps[0:w, side, 0:T], m["w1"][:, L, side * HID + at:side * HID + at + w], hnT[:], start=True, stop=True)
                    ins.then_inc(sc.filled.sem, 1)
                os_.free(pe, b, 4)
                pe.wait_ge(u_ready.sem, u_ready.after(b))
                for i in (0, 1):
                    dst = o_ps[:, i * P:(i + 1) * P]
                    pe.matmul(dst, m["ones"][0:1, :], m["b2"][0:1, L, :], start=True, stop=False)
                    for k, (at, w) in enumerate(HCH):
                        ins = pe.matmul(dst, u[0:w, k, i * P:(i + 1) * P], m["w2"][0:w, L, k, :], start=False, stop=(k == 2))
                ins.then_inc(os_.filled.sem, 1)

            skewed(pe, B, [(front, 0), (back, 1)])

        @block.scalar
        def _(act):
            act.wait_ge(consts.sem, 3)

            def front(b, par):
                if known(b, 2):
                    act.wait_ge(y1_ready.sem, y1_ready.after(b - 2))
                act.copy(y[:, par, :, :], m["xn_tok"][:, bass.ds(b * 2, 2), :]).then_inc(y_in.sem, 1)
                ft.full(act, b, 0)
                if known(b, 2):
                    act.wait_ge(qkv.filled.sem, qkv.filled.after(b - 2))
                act.copy(hT[0:64, par, :], ft_ps[0:64, 0:T])
                act.copy(hT[64:P, par, 1:T], ft_ps[64:P, 0:T - 1]).then_inc(hT_ready.sem, 1)
                act.wait_ge(hT_ready.sem, hT_ready.after(b))
                act.nop().then_inc(ft.drained.sem, 1)
                for i in (0, 1):
                    qkv.full(act, b, i)
                    if i or known(b, 1):
                        act.wait_ge(parts.sem, parts.after(b, 1) if i else parts.after(b - 1))
                    act.activation(sq[:, i, :], qkv_ps[:, 0:2, :].rearrange("p a d -> p (a d)"), ACT.Square).then_inc(sq_ready.sem, 1)
                    if known(b, 2):
                        act.wait_ge(o_ready.sem, o_ready.after(b - 2))
                    act.copy(V[:, par, i, :], qkv_ps[:, 2, :]).then_inc(qv_kept.sem, 1)
                    for w, dst in ((0, qT), (1, kT)):
                        ft.full(act, b, 1 + 2 * i + w)
                        if w == 0 and known(b, 2):
                            act.wait_ge(sc.filled.sem, sc.filled.after(b - 2))
                        act.copy(dst[:, par, :, i * P:(i + 1) * P], ft_ps[:].rearrange("p (k t) -> p k t", t=P)).then_inc(qkT_ready.sem, 1)
                        act.wait_ge(qkT_ready.sem, qkT_ready.after(b, 2 * i + w + 1))
                        act.nop().then_inc(ft.drained.sem, 1)

            def back(b, par):
                for i in (0, 1):
                    k0, k1 = KEYS[i]
                    for hf in (0, 1):
                        act.wait_ge(mx_ready.sem, mx_ready.after(b, 2 * i + hf + 1))
                        if i:
                            act.wait_ge(bt.filled.sem, bt.filled.after(b, BT[0, hf, 0] + 1))
                        elif known(b, 1):
                            act.wait_ge(bt.filled.sem, bt.filled.after(b - 1, BT[1, hf, 1] + 1))
                        for n in range(HALF):
                            h = hf * HALF + n
                            ins = act.activation(prob[:, hf, n, k0:k1], s_ps[:, h % 2, (n // 2) * 256:(n // 2) * 256 + k1 - k0], ACT.Exp,
                                                 bias=nmx[:, hf, n:n + 1], accum_out=sums[:, i, h:h + 1])
                        ins.then_inc(prob_ready.sem, 1)
                        act.wait_ge(prob_ready.sem, prob_ready.after(b, 2 * i + hf + 1))
                        act.nop().then_inc(sc.drained.sem, 1)
                    for hf in (0, 1):
                        for blk in BLOCKS[i]:
                            bt.full(act, b, BT[i, hf, blk])
                            if i:
                                act.wait_ge(os_.filled.sem, os_.filled.after(b, 1))
                            elif known(b, 1):
                                act.wait_ge(os_.filled.sem, os_.filled.after(b - 1))
                            act.copy(pT[:, hf, blk, :, :], bt_ps[:].rearrange("p (n t) -> p n t", t=P)).then_inc(pT_ready.sem, 1)
                            act.wait_ge(pT_ready.sem, pT_ready.after(b, PT[i, hf, blk] + 1))
                            act.nop().then_inc(bt.drained.sem, 1)
                    bt.full(act, b, BT[f"o{i}"])
                    act.copy(oT[:], bt_ps[:]).then_inc(oT_ready.sem, 1)
                    act.wait_ge(oT_ready.sem, oT_ready.after(b, i + 1))
                    act.nop().then_inc(bt.drained.sem, 1)
                bt.full(act, b, BT["y1"])
                act.copy(h2T[0:64, :], bt_ps[0:64, 0:T])
                act.copy(h2T[64:P, 1:T], bt_ps[64:P, 0:T - 1]).then_inc(h2T_ready.sem, 1)
                act.wait_ge(h2T_ready.sem, h2T_ready.after(b))
                act.nop().then_inc(bt.drained.sem, 1)
                bt.full(act, b, BT["hn"])
                act.activation(hnT[:], bt_ps[:, 0:T], ACT.Identity, bias=col("lnb1", L), scale=col("lng", L)).then_inc(hnT_ready.sem, 1)
                act.wait_ge(hnT_ready.sem, hnT_ready.after(b))
                act.nop().then_inc(bt.drained.sem, 1)
                for k, (at, w) in enumerate(HCH):
                    sc.full(act, b, 4 + k)
                    act.activation(gg[0:w, k, :], s_ps[0:w, 1, 0:T], ACT.Gelu, bias=col("b1g", 3 * L + k)[0:w]).then_inc(gg_ready.sem, 1)

            skewed(act, B, [(front, 0), (back, 1)])

        @block.gpsimd
        def _(pool):
            pool.tensor_copy(ident16[:], m["ident"][:]).then_inc(consts.sem, 1)
            pool.tensor_copy(mask16[:], m["mask"][:]).then_inc(consts.sem, 1)
            pool.memset(hT[:, :, 0:1], 0.0)
            pool.memset(h2T[:, 0:1], 0.0).then_inc(consts.sem, 1)
            ch = Chain(ctx, nc, pool, f"lo{L}_pool", 2)

            def rotate(b, par):
                ch.begin(b)
                for i in (0, 1):
                    pool.wait_ge(parts.sem, parts.after(b, i + 1))
                    ch.link(pool.tensor_tensor(c1[:, i, :], c1[:, i, :], c2[:, i, :], ALU.add))
                    v = c1[:, i, :].rearrange("p (h j) -> p h j", j=DH)
                    pool.tensor_tensor(v, v, rn[:, i, :].unsqueeze(2).broadcast_to([P, 2 * HEADS, DH]), ALU.mult).then_inc(rot_ready.sem, 1)
            skewed(pool, B, [(rotate, 0)])

        @block.vector
        def _(dve):
            once = Chain(ctx, nc, dve, f"lo{L}_once", 0)
            once.link(dve.tensor_tensor(tab[:].rearrange("p a c t j -> p (a c) t j"), m["rot"][:].rearrange("p a c t j -> p (a c) t j"),
                                        m["qk_scale"][:, L].rearrange("p a c j -> p (a c) j").unsqueeze(2).broadcast_to([P, 4, 2, DH]), ALU.mult))
            chf = Chain(ctx, nc, dve, f"lo{L}_dve_front", 2 * (1 + RSQRT_OPS))
            chb = Chain(ctx, nc, dve, f"lo{L}_dve_back", 2 + rownorm.links)

            def front(b, par):
                chf.begin(b)
                for i in (0, 1):
                    dve.wait_ge(sq_ready.sem, sq_ready.after(b, i + 1))
                    if known(b, 1):
                        dve.wait_ge(ft.filled.sem, ft.filled.after(b - 1, 3 + 2 * i))
                    chf.link(dve.tensor_reduce(ss[:, i, :], sq[:, i, :].rearrange("p (h j) -> p h j", j=DH), AX.X, ALU.add))
                    rsqrt(dve, chf, rn[:, i, :], ss[:, i, :], None, half[:], bits[:], aa[:], floor=1e-24)
                    pj = qkv_ps[:, 0:2, :].rearrange("p a (h j) -> p a h j", j=DH)
                    d1 = c1[:, i, :].rearrange("p (a h j) -> p a h j", a=2, j=DH)
                    d2 = c2[:, i, :].rearrange("p (a h j) -> p a h j", a=2, j=DH)
                    tb = lambda c, j0, j1: tab[:, :, c, i, j0:j1].unsqueeze(2).broadcast_to([P, 2, HEADS, j1 - j0])
                    dve.tensor_tensor(d1, pj, tb(0, 0, DH), ALU.mult)
                    H2 = DH // 2
                    dve.tensor_tensor(d2[:, :, :, 0:H2], pj[:, :, :, H2:DH], tb(1, 0, H2), ALU.mult)
                    dve.tensor_tensor(d2[:, :, :, H2:DH], pj[:, :, :, 0:H2], tb(1, H2, DH), ALU.mult).then_inc(parts.sem, 1)
                    dve.wait_ge(parts.sem, parts.after(b, i + 1))
                    dve.wait_ge(qv_kept.sem, qv_kept.after(b, i + 1))
                    dve.nop().then_inc(qkv.drained.sem, 1)
                chf.end()

            def back(b, par):
                chb.begin(b)
                for i in (0, 1):
                    k0, k1 = KEYS[i]
                    for hf in (0, 1):
                        sc.full(dve, b, 2 * i + hf)
                        v = s_ps[:].rearrange("p k (a w) -> p a k w", w=256)[:, :, :, 0:k1 - k0]
                        if i:
                            dve.wait_ge(prob_ready.sem, prob_ready.after(b, 2 * (i - 1) + hf + 1))
                        elif known(b, 1):
                            dve.wait_ge(prob_ready.sem, prob_ready.after(b - 1))
                        dve.tensor_reduce(nmx[:, hf, :].rearrange("p (a k) -> p a k", k=2), v, AX.X, ALU.max, negate=True).then_inc(mx_ready.sem, 1)
                    dve.wait_ge(prob_ready.sem, prob_ready.after(b, 2 * i + 2))
                    chb.link(dve.reciprocal(rsum[:], sums[:, i, :]))
                    os_.full(dve, b, 2 * i)
                    if i:
                        dve.wait_ge(bt.filled.sem, bt.filled.after(b, BT["o0"] + 1))
                    elif known(b, 1):
                        dve.wait_ge(bt.filled.sem, bt.filled.after(b - 1, BT["o1"] + 1))
                    dve.tensor_tensor(o[:].rearrange("p (h j) -> p h j", j=DH), o_ps[:].rearrange("p (h j) -> p h j", j=DH),
                                      rsum[:].unsqueeze(2).broadcast_to([P, HEADS, DH]), ALU.mult).then_inc(o_ready.sem, 1)
                    dve.wait_ge(o_ready.sem, o_ready.after(b, i + 1))
                    dve.nop().then_inc(os_.drained.sem, 1)
                    os_.full(dve, b, 2 * i + 1)
                    dve.tensor_tensor(y1[:, i, :], y[:, par, i, :], o_ps[:, 0:D], ALU.add).then_inc(y1_ready.sem, 1)
                    dve.wait_ge(y1_ready.sem, y1_ready.after(b, i + 1))
                    dve.nop().then_inc(os_.drained.sem, 1)
                bt.full(dve, b, BT["h2"])
                if known(b, 1):
                    dve.wait_ge(bt.filled.sem, bt.filled.after(b - 1, BT["hn"] + 1))
                rownorm(dve, chb, lambda j: bt_ps[:, j * P:(j + 1) * P], lambda j: hn[:, j, :], hn_ready)
                dve.wait_ge(hn_ready.sem, hn_ready.after(b))
                dve.nop().then_inc(bt.drained.sem, 1)
                for k, (at, w) in enumerate(HCH):
                    dve.wait_ge(gg_ready.sem, gg_ready.after(b, k + 1))
                    dve.scalar_tensor_tensor(u[0:w, k, :], s_ps[0:w, 0, 0:T], col("b1a", 3 * L + k)[0:w], gg[0:w, k, :], ALU.add, ALU.mult).then_inc(u_ready.sem, 1)
                    dve.wait_ge(u_ready.sem, u_ready.after(b, k + 1))
                    dve.nop().then_inc(sc.drained.sem, 1)
                os_.full(dve, b, 4)
                dve.tensor_tensor(m["xn_tok"][:, bass.ds(b * 2, 2), :], y1[:], o_ps[:, 0:2 * D].rearrange("p (a d) -> p a d", d=D), ALU.add).then_inc(y2_ready.sem, 1)
                dve.wait_ge(y2_ready.sem, y2_ready.after(b))
                dve.nop().then_inc(os_.drained.sem, 1)
                chb.end()

            skewed(dve, B, [(front, 0), (back, 1)])


def finish_phase(nc, m, out):
    with Phase(nc) as ctx:
        sb = lambda n, s, d=F32: ctx.enter_context(nc.sbuf_tensor(n, s, d))
        st = lambda n, per=1: Step(ctx, nc, n, per)
        g_, sg, x2 = (sb("fi_" + k, [P, 2, GT, D]) for k in ("g", "sg", "x2"))
        g_ready, x2_ready = st("fi_g_ready"), st("fi_x2_ready")
        stored = [st(f"fi_stored{k}", 16) for k in (0, 1)]
        block = ctx.block()
        grp = lambda name, g: m[name][:, bass.ds(g * GT, GT), :]
        dst = out.rearrange("(n p) d -> p n d", p=P)

        @block.scalar
        def _(act):
            def fn(g, par):
                if known(g, 2):
                    act.wait_ge(x2_ready.sem, x2_ready.after(g - 2))
                act.activation(g_[:, par, :, :], grp("xn_tok", g), ACT.Silu).then_inc(g_ready.sem, 1)
            skewed(act, NG, [(fn, 0)])

        @block.vector
        def _(dve):
            ch = Chain(ctx, nc, dve, "fi_dve", 1)

            def fn(g, par):
                ch.begin(g)
                dve.wait_ge(g_ready.sem, g_ready.after(g))
                if known(g, 2):
                    dve.wait_ge(stored[par].sem, (g - par) * 8)
                ch.link(dve.tensor_tensor(sg[:, par, :, :], g_[:, par, :, :], grp("s1_tok", g), ALU.mult))
                dve.tensor_tensor(x2[:, par, :, :], sg[:, par, :, :], grp("x_tok", g), ALU.add).then_inc(x2_ready.sem, 1)
            skewed(dve, NG, [(fn, 0)])

        @block.sync
        def _(sp):
            def fn(g, par):
                sp.wait_ge(x2_ready.sem, x2_ready.after(g))
                sp.dma_start(dst[:, bass.ds(g * GT, GT), :], x2[:, par, :, :]).then_inc(stored[par].sem, 16)
            skewed(sp, NG, [(fn, 0)])
            for par in (0, 1):
                sp.wait_ge(stored[par].sem, 16 * (NG // 2))


def layer1(nc, m, a, out):
    with ExitStack() as ctx:
        s1 = ctx.enter_context(nc.sbuf_tensor("s1_tok", [P, NT, D], F32))
        with ExitStack() as c:
            m1 = dict(m, s1_tok=s1)
            for k in ("qT", "kT", "kabT", "bvT", "aT"):
                m1[k] = c.enter_context(nc.sbuf_tensor(k, [P, B, T], F32))
            with ExitStack() as c2:
                names = ["WqT", "WkT", "WvT", "conv_q", "conv_k", "conv_v", "WaP", "WbP", "dt_compact", "head_mat", "group_mat"]
                for k in names:
                    m1[k] = c2.enter_context(nc.sbuf_tensor(k, SHAPES1[k], F32))
                m1["loads"] = names
                load_phase(nc, m1, a)
                prepare_phase(nc, m1)
            with ExitStack() as c2:
                m1["spread_mat"] = c2.enter_context(nc.sbuf_tensor("spread_mat", SHAPES1["spread_mat"], F32))
                m1["loads"] = ["spread_mat"]
                load_phase(nc, m1, a)
                delta_phase(nc, m1)
            with ExitStack() as c2:
                names = ["head_mean", "WgT", "WoT"]
                for k in names:
                    m1[k] = c2.enter_context(nc.sbuf_tensor(k, SHAPES1[k], F32))
                m1["loads"] = names
                load_phase(nc, m1, a)
                delta_out_phase(nc, m1)
        m2 = dict(m, s1_tok=s1)
        for k, s in SHAPES2.items():
            m2[k] = ctx.enter_context(nc.sbuf_tensor(k, s, F32))
        m2["loads"] = list(SHAPES2)
        load_phase(nc, m2, a)
        for layer in range(LAYERS):
            local_phase(nc, m2, layer)
        finish_phase(nc, m2, out)


def feature_cols(a, n):
    return np.ascontiguousarray(a.reshape(n, P).T)


def pad_col(a):
    out = np.zeros((P, 1), a.dtype)
    out[:a.shape[0], 0] = a
    return out


def lay_out(v):
    f = np.float32
    a = {}
    a["x"] = v["L0_attn_x"].reshape(B * T, D)
    a["lnw0"] = np.broadcast_to(v["L0_attn_ln_w"][None], (P, D))
    a["lnb0"] = np.broadcast_to(v["L0_attn_ln_b"][None], (P, D))
    a["bo0"] = v["L0_attn_b"][None, 2 * D:3 * D]
    a["W0T"] = v["L0_attn_W"].T
    w_in = v["L0_ffn_W_in"].reshape(TREES, -1, FAN, D)
    w_out = v["L0_ffn_W_out"].T.reshape(TREES, -1, FAN, D)
    b_in = v["L0_ffn_b_in"].reshape(TREES, -1, FAN)
    at = [(FAN ** d - 1) // (FAN - 1) for d in range(DEPTH + 2)]
    lv = lambda w, d: w[:, at[d]:at[d + 1]]
    top_in = np.concatenate([lv(w_in, d).reshape(-1, D) for d in range(TOP)])
    top_out = np.concatenate([lv(w_out, d).reshape(-1, D) for d in range(TOP)] + [np.zeros((TCH * P - TOPW, D), f)])
    a["top_in"] = top_in.T
    a["top_out"] = top_out.reshape(TCH, P, D).transpose(1, 0, 2)
    a["top_b"] = np.concatenate([lv(b_in, d).reshape(-1) for d in range(TOP)])[None]
    for d in (4, 5):
        n = TREES * FAN ** d
        a[f"table{d}"] = np.concatenate([lv(w_in, d).reshape(n, -1), lv(w_out, d).reshape(n, -1), lv(b_in, d).reshape(n, -1)], axis=1)
    for k, w in (("q", "L1_attn_Wq"), ("k", "L1_attn_Wk"), ("v", "L1_attn_Wv")):
        a[f"W{k}T"] = v[w].T
        a[f"conv_{k}"] = np.broadcast_to(v[f"L1_attn_conv_{k}"].T[None], (P, TAPS, P))
    for k in "ab":
        w = np.zeros((P, NG, NG, NH), f)
        for g in range(NG):
            w[:, g, g, :] = v[f"L1_attn_W{k}"].T
        a[f"W{k}P"] = w.reshape(P, NG, P)
    a["dt_compact"] = np.stack([np.tile(v["L1_attn_dt_bias"], NG), np.tile(v["L1_attn_A_log"], NG)], axis=1)
    a["WgT"], a["WoT"] = v["L1_attn_Wg"].T, v["L1_attn_Wo"].T
    b1 = v["L1_ffn_b1"]
    cols = [feature_cols(v["L0_attn_b"], 4), v["L0_attn_ln_w"][:, None], v["L0_attn_ln_b"][:, None],
            np.full((P, 1), 1e-6, f), np.full((P, 1), EPS, f), np.tile(v["L1_attn_norm_w"], NH)[:, None],
            v["L1_ffn_ln_g"].T, v["L1_ffn_ln_b"].T]
    for o in (0, HID):
        cols += [pad_col(b1[l, o + c:o + c + w]) for l in range(LAYERS) for c, w in HCH]
    a["cols"] = np.concatenate(cols, axis=1)
    a["wqkv"] = v["L1_ffn_wqkv"].transpose(1, 0, 2)
    a["wo"] = v["L1_ffn_wo"].reshape(LAYERS, INNER // P, P, D).transpose(2, 0, 1, 3)
    a["w1"] = v["L1_ffn_w1"].transpose(1, 0, 2)
    w2 = np.concatenate([v["L1_ffn_w2"], np.zeros((LAYERS, len(HCH) * P - HID, D), f)], axis=1)
    a["w2"] = w2.reshape(LAYERS, len(HCH), P, D).transpose(2, 0, 1, 3)
    a["b2"] = v["L1_ffn_b2"][None]
    sc = np.stack([v["L1_ffn_q_scale"], v["L1_ffn_k_scale"]], axis=1)
    sc = np.stack([sc, np.concatenate([sc[..., DH // 2:], sc[..., :DH // 2]], axis=-1)], axis=2)
    a["qk_scale"] = np.broadcast_to(sc[None], (P,) + sc.shape)
    a["ident"] = np.eye(P, dtype=f)
    a["head_mat"] = np.kron(np.eye(NH, dtype=f), np.ones((HD, HD), f))
    a["head_mean"] = a["head_mat"] / HD
    a["group_mat"] = np.stack([np.kron(np.outer(np.eye(NG, dtype=f)[g], np.ones(1, f))[:, None, :].reshape(NG, 1), np.kron(np.eye(NH, dtype=f), np.ones((1, HD), f))) for g in range(NG)], axis=1)
    a["spread_mat"] = np.stack([np.kron(np.eye(NH, dtype=f), np.outer(np.eye(HD, dtype=f)[d], np.ones(HD, f))) for d in range(HD)], axis=1)
    a["ones"] = np.ones((1, P), f)
    a["iota"] = np.broadcast_to(np.arange(FAN ** (TOP - 1), dtype=f)[None], (P, FAN ** (TOP - 1)))
    a["first"] = np.broadcast_to(np.tile(np.arange(FAN, 0, -1, dtype=f), TREES)[None], (P, PICK))
    a["four"] = np.full((P, TREES), float(FAN), f)
    a["base4"] = np.broadcast_to(np.arange(TREES, dtype=f)[None] * FAN ** 4, (P, TREES))
    a["base5"] = np.broadcast_to(np.arange(TREES, dtype=f)[None] * FAN ** 5, (P, TREES))
    half = np.arange(0, DH, 2, dtype=f)
    t = np.arange(T, dtype=f)
    freq = t[:, None] * (f(1.0) / f(10000.0) ** (half / f(DH)))[None]
    freq = np.concatenate([freq, freq], axis=-1)
    base = (half + f(0.4 * DH)) / f(1.4 * DH)
    scale = base[None] ** ((t - T // 2) / f(WIN // 2))[:, None]
    scale = np.concatenate([scale, scale], axis=-1)
    sign = np.concatenate([-np.ones(DH // 2, f), np.ones(DH // 2, f)])
    cos, sin = np.cos(freq), np.sin(freq) * sign
    rot = np.stack([np.stack([8 * cos * scale, 8 * sin * scale]), np.stack([cos / scale, sin / scale])])
    a["rot"] = rot.reshape(2, 2, 2, P, DH).transpose(3, 0, 1, 2, 4)
    i, j = np.arange(T)[:, None], np.arange(T)[None]
    a["mask"] = np.where((i < j) | (i > j + WIN) | (j // WIN < i // WIN - 1), f(MASKED), f(0)).reshape(2, P, T).transpose(1, 0, 2)
    return {k: np.ascontiguousarray(np.asarray(x, f)) for k, x in a.items()}


SHAPES = dict(
    W0T=[P, 4 * P], lnw0=[P, D], lnb0=[P, D], bo0=[1, D], top_in=[P, TOPW], top_out=[P, TCH, D], top_b=[1, TOPW], cols=[P, NCOL],
    ident=[P, P], ones=[1, P], iota=[P, FAN ** (TOP - 1)], first=[P, PICK],
    four=[P, TREES], base4=[P, TREES], base5=[P, TREES])
SHAPES1 = dict(
    WqT=[P, P], WkT=[P, P], WvT=[P, P], conv_q=[P, TAPS, P], conv_k=[P, TAPS, P], conv_v=[P, TAPS, P],
    WbP=[P, NG, P], WaP=[P, NG, P], dt_compact=[P, 2], group_mat=[P, NG, P], WgT=[P, P], WoT=[P, P], head_mat=[P, P], head_mean=[P, P], spread_mat=[P, HD, P])
SHAPES2 = dict(
    wqkv=[P, LAYERS, 3 * INNER], wo=[P, LAYERS, INNER // P, D], w1=[P, LAYERS, 2 * HID],
    w2=[P, LAYERS, len(HCH), D], b2=[1, LAYERS, D], qk_scale=[P, LAYERS, 2, 2, DH], rot=[P, 2, 2, 2, DH],
    mask=[P, 2, T])


def program(nc, a, out):
    tok = lambda ap: ap.rearrange("(n p) d -> p n d", p=P)

    with ExitStack() as keep:
        res = lambda k, s: keep.enter_context(nc.sbuf_tensor(k, s, F32))
        m = {k: res(k, s) for k, s in dict(cols=[P, NCOL], ident=[P, P], ones=[1, P], x_tok=[P, NT, D], xn_tok=[P, NT, D], xT_pad=[P, B, PADT]).items()}
        with ExitStack() as layer0:
            m0 = dict(m)
            for k, s in dict(SHAPES, s_tok=[P, NT, D], f_tok=[P, NT, D], rel_all=[P, NT, TREES]).items():
                if k not in m0:
                    m0[k] = layer0.enter_context(nc.sbuf_tensor(k, s, F32))
            m0["loads"] = list(SHAPES) + ["x_tok"]
            load_phase(nc, m0, dict(a, x_tok=tok(a["x"])))
            gates_phase(nc, m0)
            tree_top_phase(nc, m0)
            tree_deep_phase(nc, m0, a["table4"], a["table5"])
            merge_phase(nc, m0)
            m = {k: m0[k] for k in ("cols", "ident", "ones", "x_tok", "xn_tok", "xT_pad")}
        layer1(nc, m, a, out)


def kernel(**inputs):
    import concourse.bacc as bacc
    from concourse.bass_utils import run_bass_kernel_spmd

    host = lay_out({k: np.asarray(x) for k, x in inputs.items()})
    nc = bacc.Bacc("TRN2", target_bir_lowering=False, num_devices=1)
    a = {k: nc.dram_tensor("in_" + k, x.shape, F32, kind="ExternalInput").ap() for k, x in host.items()}
    out = nc.dram_tensor("out", (B * T, D), F32, kind="ExternalOutput").ap()
    program(nc, a, out)
    r = run_bass_kernel_spmd(nc, [{"in_" + k: x for k, x in host.items()}], core_ids=[0])
    return r.results[0]["out"].reshape(B, T, D)
```
